# Optimizing a Trainium2 kernel written in Bass

```python
import numpy as np
import jax
import jax.numpy as jnp

def _softmax(x, axis=-1):
    return jax.nn.softmax(x, axis=axis)

def _gelu(x):
    return jax.nn.gelu(x, approximate=True)

def _silu(x):
    return jax.nn.silu(x)

def _sigmoid(x):
    return jax.nn.sigmoid(x)

def _layernorm(x, axis=-1, eps=1e-05):
    m = jnp.mean(x, axis=axis, keepdims=True)
    v = jnp.var(x, axis=axis, keepdims=True)
    return (x - m) / jnp.sqrt(v + eps)

def _scatter_add(tgt, idx, src, axis=0):
    return tgt.at[idx].add(src)

def _segment_sum(src, seg, n):
    return jax.ops.segment_sum(src, seg, n)
kernel_name = 'mk_perceiver_d1_seqx_r8_d9bcdb'

def setup_inputs(seed: int=0):
    np.random.seed(seed)
    _w = jnp.asarray

    def _rec_inputs():
        import jax
        import jax.numpy as jnp
        _rk = jax.random.key(seed)
        x = -0.0002928 + 1 * jax.random.normal(jax.random.fold_in(_rk, 1), (64, 32, 128), jnp.float32)
        _lenS = 32 - jax.random.randint(jax.random.fold_in(_rk, 7), (64,), 0, max(1, 32 // 4) + 1, jnp.int32)
        _lenS2 = 257 - jax.random.randint(jax.random.fold_in(_rk, 8), (64,), 0, max(1, 257 // 4) + 1, jnp.int32)
        _ctx_1024P = jax.random.normal(jax.random.fold_in(_rk, 11), (64, 16, 128), jnp.float32)
        _ctx_1024c = jax.random.dirichlet(jax.random.fold_in(_rk, 511), 0.3 * jnp.ones((16,), jnp.float32), (64, 257))
        _ctx_1024t = jnp.einsum('bsk,bkd->bsd', _ctx_1024c, _ctx_1024P)
        _ctx_1024t = _ctx_1024t * jax.lax.rsqrt(jnp.mean(jnp.square(_ctx_1024t)) + 1e-12) * 0.953939
        ctx_1024 = -1.39393e-06 + 0.999914 * (_ctx_1024t + 0.3 * jax.random.normal(jax.random.fold_in(_rk, 611), (64, 257, 128), jnp.float32))
        return (x, ctx_1024)
    x, ctx_1024 = _rec_inputs()

    def _L0_xattn_setup():
        import jax, jax.numpy as jnp
        import numpy as np
        D_MODEL = 128
        NHEAD = 16
        HEAD_DIM = D_MODEL // NHEAD
        key = jax.random.key(seed)
        ks = jax.random.split(key, 11)
        B, S = (2, 256)
        scale = 1.0 / np.sqrt(D_MODEL)
        inp = {'query': jax.random.normal(ks[0], (B, S, D_MODEL), jnp.float32), 'key': jax.random.normal(ks[1], (B, S, D_MODEL), jnp.float32), 'value': jax.random.normal(ks[2], (B, S, D_MODEL), jnp.float32), 'Wq': jax.random.normal(ks[3], (D_MODEL, D_MODEL), jnp.float32) * scale, 'bq': jnp.zeros((D_MODEL,), jnp.float32), 'Wk': jax.random.normal(ks[4], (D_MODEL, D_MODEL), jnp.float32) * scale, 'bk': jnp.zeros((D_MODEL,), jnp.float32), 'Wv': jax.random.normal(ks[5], (D_MODEL, D_MODEL), jnp.float32) * scale, 'bv': jnp.zeros((D_MODEL,), jnp.float32), 'Wo': jax.random.normal(ks[6], (D_MODEL, D_MODEL), jnp.float32) * scale, 'bo': jnp.zeros((D_MODEL,), jnp.float32)}
        return inp
    _L0_xattn_all = _L0_xattn_setup()
    _L0_xattn_in = {k: v for k, v in _L0_xattn_all.items() if k in ('Wq', 'bq', 'Wk', 'bk', 'Wv', 'bv', 'Wo', 'bo')}
    del _L0_xattn_all

    def _L0_attn_setup():
        import jax, jax.numpy as jnp
        import numpy as np
        DIM = 128
        D_INNER = 128
        N_STATE = 32
        N_BLOCKS = 4
        TOP_K = 2
        ROUTER_TEMP = 1.0
        INIT_BETA_BIAS = 2.0
        BATCH = 16
        T = 256

        def _xavier(key, shape):
            fan_out, fan_in = shape
            lim = jnp.sqrt(6.0 / (fan_in + fan_out))
            return jax.random.uniform(key, shape, jnp.float32, -lim, lim)

        def _cell_scan(x_rnn, W_router, W_kv, W_beta, b_beta, W_q):
            Tt, batch, D = x_rnn.shape
            n, nb = (N_STATE, N_BLOCKS)
            xf = x_rnn.reshape(Tt * batch, D)
            logits = (xf @ W_router.T).reshape(Tt, batch, nb) / ROUTER_TEMP
            kv = (xf @ W_kv.T).reshape(Tt, batch, nb, 2, n)
            beta = jax.nn.sigmoid((xf @ W_beta.T).reshape(Tt, batch, nb, n) + b_beta)
            q = (xf @ W_q.T).reshape(Tt, batch, n)
            S0 = jnp.zeros((batch, nb, n, n), x_rnn.dtype)
            rows = jnp.arange(batch)[:, None]

            def step(S, inp):
                logits_t, k_t, v_t, beta_t, q_t = inp
                _, idx = jax.lax.top_k(logits_t, TOP_K)
                mask = jnp.zeros_like(logits_t).at[rows, idx].set(1.0)
                sm = jax.nn.softmax(logits_t, axis=-1)
                uw = mask * sm
                uw = uw / (uw.sum(-1, keepdims=True) + 1e-08)
                kn = k_t / (jnp.linalg.norm(k_t, axis=-1, keepdims=True) + 1e-06)
                retrieved = jnp.einsum('bnij,bnj->bni', S, kn)
                delta = v_t - retrieved
                outer = delta[..., :, None] * kn[..., None, :]
                S_upd = jnp.tanh(beta_t[..., None] * S + outer)
                w = uw[..., None, None]
                S_new = (1.0 - w) * S + w * S_upd
                Sq = jnp.einsum('bnij,bj->bni', S_new, q_t)
                block_out = Sq * (Sq * jax.nn.sigmoid(Sq))
                out_t = jnp.einsum('bn,bnd->bd', sm, block_out)
                return (S_new, out_t)
            S_final, outs = jax.lax.scan(step, S0, (logits, kv[..., 0, :], kv[..., 1, :], beta, q))
            return (outs, S_final)

        def _reference_tuple_inner(x, W_in, W_router, W_kv, W_beta, b_beta, W_q, W_out):
            x_proj = jax.nn.silu(x @ W_in.T)
            x_rnn = jnp.transpose(x_proj, (1, 0, 2))
            cell_out, S_final = _cell_scan(x_rnn, W_router, W_kv, W_beta, b_beta, W_q)
            y = jnp.transpose(cell_out, (1, 0, 2)) @ W_out.T
            return (y, S_final)
        key = jax.random.key(seed)
        ks = jax.random.split(key, 7)
        x = jax.random.normal(ks[0], (BATCH, T, DIM), jnp.float32)
        W_in = _xavier(ks[1], (D_INNER, DIM))
        W_router = _xavier(ks[2], (N_BLOCKS, D_INNER))
        W_kv = _xavier(ks[3], (N_BLOCKS * 2 * N_STATE, D_INNER))
        W_beta = _xavier(ks[4], (N_BLOCKS * N_STATE, D_INNER))
        b_beta = jnp.full((N_BLOCKS, N_STATE), INIT_BETA_BIAS, jnp.float32)
        W_q = _xavier(ks[5], (N_STATE, D_INNER))
        W_out = _xavier(ks[6], (DIM, N_STATE))
        return {'x': x, 'W_in': W_in, 'W_router': W_router, 'W_kv': W_kv, 'W_beta': W_beta, 'b_beta': b_beta, 'W_q': W_q, 'W_out': W_out}
    _L0_attn_all = _L0_attn_setup()
    _L0_attn_in = {k: v for k, v in _L0_attn_all.items() if k in ('W_in', 'W_router', 'W_kv', 'W_beta', 'b_beta', 'W_q', 'W_out')}
    del _L0_attn_all

    def _L0_ffn_setup():
        import jax, jax.numpy as jnp
        import numpy as np
        B, S, D, E, F = (2, 256, 128, 8, 512)
        key = jax.random.key(seed)
        ks = jax.random.split(key, 4)
        return {'hidden_states': jax.random.normal(ks[0], (B, S, D), dtype=jnp.float32), 'Wr': jax.random.normal(ks[1], (D, E), dtype=jnp.float32) * (1.0 / np.sqrt(D)), 'W1': jax.random.normal(ks[2], (E, D, F), dtype=jnp.float32) * (1.0 / np.sqrt(D)), 'b1': jnp.zeros((E, F), dtype=jnp.float32), 'W2': jax.random.normal(ks[3], (E, F, D), dtype=jnp.float32) * (1.0 / np.sqrt(F)), 'b2': jnp.zeros((E, D), dtype=jnp.float32)}
    _L0_ffn_all = _L0_ffn_setup()
    _L0_ffn_in = {k: v for k, v in _L0_ffn_all.items() if k in ('Wr', 'W1', 'b1', 'W2', 'b2')}
    del _L0_ffn_all
    return {'x': x, 'ctx_1024': ctx_1024, 'L0_xattn_Wq': _L0_xattn_in['Wq'], 'L0_xattn_bq': _L0_xattn_in['bq'], 'L0_xattn_Wk': _L0_xattn_in['Wk'], 'L0_xattn_bk': _L0_xattn_in['bk'], 'L0_xattn_Wv': _L0_xattn_in['Wv'], 'L0_xattn_bv': _L0_xattn_in['bv'], 'L0_xattn_Wo': _L0_xattn_in['Wo'], 'L0_xattn_bo': _L0_xattn_in['bo'], 'L0_attn_W_in': _L0_attn_in['W_in'], 'L0_attn_W_router': _L0_attn_in['W_router'], 'L0_attn_W_kv': _L0_attn_in['W_kv'], 'L0_attn_W_beta': _L0_attn_in['W_beta'], 'L0_attn_b_beta': _L0_attn_in['b_beta'], 'L0_attn_W_q': _L0_attn_in['W_q'], 'L0_attn_W_out': _L0_attn_in['W_out'], 'L0_ffn_Wr': _L0_ffn_in['Wr'], 'L0_ffn_W1': _L0_ffn_in['W1'], 'L0_ffn_b1': _L0_ffn_in['b1'], 'L0_ffn_W2': _L0_ffn_in['W2'], 'L0_ffn_b2': _L0_ffn_in['b2']}

def reference(x, ctx_1024, L0_xattn_Wq, L0_xattn_bq, L0_xattn_Wk, L0_xattn_bk, L0_xattn_Wv, L0_xattn_bv, L0_xattn_Wo, L0_xattn_bo, L0_attn_W_in, L0_attn_W_router, L0_attn_W_kv, L0_attn_W_beta, L0_attn_b_beta, L0_attn_W_q, L0_attn_W_out, L0_ffn_Wr, L0_ffn_W1, L0_ffn_b1, L0_ffn_W2, L0_ffn_b2):
    import jax
    import jax.numpy as jnp

    def _L0_xattn_ref(query, key, value, Wq, bq, Wk, bk, Wv, bv, Wo, bo):
        import jax, jax.numpy as jnp
        import numpy as np
        D_MODEL = 128
        NHEAD = 16
        HEAD_DIM = D_MODEL // NHEAD
        B, S, _ = query.shape

        def proj(x, W, b):
            y = x @ W.T + b
            return y.reshape(B, -1, NHEAD, HEAD_DIM).transpose(0, 2, 1, 3)
        q = proj(query, Wq, bq)
        k = proj(key, Wk, bk)
        v = proj(value, Wv, bv)
        scores = jnp.einsum('bhqd,bhkd->bhqk', q, k) / np.sqrt(HEAD_DIM)
        attn = jax.nn.softmax(scores, axis=-1)
        out = jnp.einsum('bhqk,bhkd->bhqd', attn, v)
        out = out.transpose(0, 2, 1, 3).reshape(B, S, D_MODEL)
        return out @ Wo.T + bo

    def _L0_attn_ref(x, W_in, W_router, W_kv, W_beta, b_beta, W_q, W_out):
        import jax, jax.numpy as jnp
        import numpy as np
        DIM = 128
        D_INNER = 128
        N_STATE = 32
        N_BLOCKS = 4
        TOP_K = 2
        ROUTER_TEMP = 1.0
        INIT_BETA_BIAS = 2.0
        BATCH = 16
        T = 256

        def _xavier(key, shape):
            fan_out, fan_in = shape
            lim = jnp.sqrt(6.0 / (fan_in + fan_out))
            return jax.random.uniform(key, shape, jnp.float32, -lim, lim)

        def _cell_scan(x_rnn, W_router, W_kv, W_beta, b_beta, W_q):
            Tt, batch, D = x_rnn.shape
            n, nb = (N_STATE, N_BLOCKS)
            xf = x_rnn.reshape(Tt * batch, D)
            logits = (xf @ W_router.T).reshape(Tt, batch, nb) / ROUTER_TEMP
            kv = (xf @ W_kv.T).reshape(Tt, batch, nb, 2, n)
            beta = jax.nn.sigmoid((xf @ W_beta.T).reshape(Tt, batch, nb, n) + b_beta)
            q = (xf @ W_q.T).reshape(Tt, batch, n)
            S0 = jnp.zeros((batch, nb, n, n), x_rnn.dtype)
            rows = jnp.arange(batch)[:, None]

            def step(S, inp):
                logits_t, k_t, v_t, beta_t, q_t = inp
                _, idx = jax.lax.top_k(logits_t, TOP_K)
                mask = jnp.zeros_like(logits_t).at[rows, idx].set(1.0)
                sm = jax.nn.softmax(logits_t, axis=-1)
                uw = mask * sm
                uw = uw / (uw.sum(-1, keepdims=True) + 1e-08)
                kn = k_t / (jnp.linalg.norm(k_t, axis=-1, keepdims=True) + 1e-06)
                retrieved = jnp.einsum('bnij,bnj->bni', S, kn)
                delta = v_t - retrieved
                outer = delta[..., :, None] * kn[..., None, :]
                S_upd = jnp.tanh(beta_t[..., None] * S + outer)
                w = uw[..., None, None]
                S_new = (1.0 - w) * S + w * S_upd
                Sq = jnp.einsum('bnij,bj->bni', S_new, q_t)
                block_out = Sq * (Sq * jax.nn.sigmoid(Sq))
                out_t = jnp.einsum('bn,bnd->bd', sm, block_out)
                return (S_new, out_t)
            S_final, outs = jax.lax.scan(step, S0, (logits, kv[..., 0, :], kv[..., 1, :], beta, q))
            return (outs, S_final)

        def _reference_tuple_inner(x, W_in, W_router, W_kv, W_beta, b_beta, W_q, W_out):
            x_proj = jax.nn.silu(x @ W_in.T)
            x_rnn = jnp.transpose(x_proj, (1, 0, 2))
            cell_out, S_final = _cell_scan(x_rnn, W_router, W_kv, W_beta, b_beta, W_q)
            y = jnp.transpose(cell_out, (1, 0, 2)) @ W_out.T
            return (y, S_final)
        return _reference_tuple_inner(x, W_in, W_router, W_kv, W_beta, b_beta, W_q, W_out)[0]

    def _L0_ffn_ref(hidden_states, Wr, W1, b1, W2, b2):
        import jax, jax.numpy as jnp
        import numpy as np
        B, S, D, E, F = (2, 256, 128, 8, 512)
        b, s, d = hidden_states.shape
        e = Wr.shape[1]
        x = hidden_states.reshape(b * s, d)
        router_logits = x @ Wr
        router_probs = jax.nn.softmax(router_logits, axis=-1)
        expert_idx = jnp.argmax(router_probs, axis=-1)
        p_max = jnp.max(router_probs, axis=-1, keepdims=True)

        def expert_mlp(w1, bb1, w2, bb2):
            h = jax.nn.gelu(x @ w1 + bb1, approximate=False)
            return h @ w2 + bb2
        outs = jax.vmap(expert_mlp)(W1, b1, W2, b2)
        onehot = jax.nn.one_hot(expert_idx, e, dtype=x.dtype)
        next_states = jnp.einsum('te,etd->td', onehot, outs)
        out = p_max * next_states
        return out.reshape(b, s, d)
    x = x + _L0_xattn_ref(_layernorm(x, axis=-1), ctx_1024, ctx_1024, L0_xattn_Wq, L0_xattn_bq, L0_xattn_Wk, L0_xattn_bk, L0_xattn_Wv, L0_xattn_bv, L0_xattn_Wo, L0_xattn_bo)
    x = x + _L0_attn_ref(_layernorm(x, axis=-1), L0_attn_W_in, L0_attn_W_router, L0_attn_W_kv, L0_attn_W_beta, L0_attn_b_beta, L0_attn_W_q, L0_attn_W_out)
    x = x + _L0_ffn_ref(_layernorm(x, axis=-1), L0_ffn_Wr, L0_ffn_W1, L0_ffn_b1, L0_ffn_W2, L0_ffn_b2)
    return x

_drawn_inputs = setup_inputs


def setup_inputs(seed=0):
    import zlib

    import numpy as np

    out = dict(_drawn_inputs(seed))
    spreads = {'L0_xattn_bq': (0.0, 0.1),
     'L0_xattn_bk': (0.0, 0.8),
     'L0_xattn_bv': (0.0, 0.1),
     'L0_xattn_bo': (0.0, 0.1),
     'L0_attn_b_beta': (2.0, 0.2),
     'L0_ffn_b1': (0.0, 0.375),
     'L0_ffn_b2': (0.0, 0.1)}
    factors = {}
    for name, (base, spread) in spreads.items():
        noise = np.random.default_rng([zlib.crc32(name.encode()), seed]).standard_normal(out[name].shape)
        drawn = base * np.exp(spread * noise) if base else spread * noise
        out[name] = jnp.asarray(drawn.astype(out[name].dtype))
    for name, factor in factors.items():
        out[name] = (out[name] * factor).astype(out[name].dtype)
    return out
```

```python
from contextlib import ExitStack

import numpy as np

import concourse.bass as bass
from concourse import mybir

NB = 64
T = 32
D = 128
TOK = NB * T
S_CTX = 257
KCH = 86
NCH = 3
S_PAD = KCH * NCH
H = 16
DH = D // H
HG = 4
NG = H // HG
N_ST = 32
BLK = 4
G2 = 2
ST = N_ST * N_ST
ROWF = 2 * N_ST * 3 + N_ST + BLK
E = 8
F = 512
FC = F // D
CH = 512
NC = TOK // CH
TT = TOK // D

_COLS = [("wq", D), ("wk", D), ("wv", D), ("wo", D), ("win", D), ("wrow0", ROWF), ("wrow1", ROWF), ("wr", E),
         ("ident", D), ("mean", D), ("head_of_row", HG), ("own_head", HG), ("sum_heads", T), ("sum_halves", NB),
         ("bq", 1), ("bk", 1), ("bv", 1), ("bo", 1), ("bbeta", G2 * N_ST), ("wout", D), ("low4", 16), ("up4", 16),
         ("low8", 64), ("b1", E * FC), ("b2", D), ("eps", 1)]
COL, _at = {}, 0
for _n, _w in _COLS:
    COL[_n] = (_at, _at + _w)
    _at += _w
NCONST = _at


def build(nc, xT, ctxT, cst_d, w1_d, w2_d, out_d):
    fp32 = mybir.dt.float32
    ALU = mybir.AluOpType
    ACT = mybir.ActivationFunctionType
    AX = mybir.AxisListType

    with ExitStack() as ctx:
        def sb(name, shape):
            return ctx.enter_context(nc.sbuf_tensor(name, shape, fp32))

        def sem(name):
            return ctx.enter_context(nc.semaphore(name))

        bank = [ctx.enter_context(nc.psum_tensor(f"bank{i}", [128, 512], fp32)) for i in range(4)]
        pair = [ctx.enter_context(nc.psum_tensor(f"pair{i}", [128, 2, 512], fp32)) for i in range(2)]
        bank += [pair[0][:, 0, :], pair[0][:, 1, :], pair[1][:, 0, :], pair[1][:, 1, :]]

        cst = sb("cst", [128, NCONST])

        def C(name):
            return cst[:, COL[name][0]:COL[name][1]]

        x = sb("x", [D, TOK])
        xc = sb("xc", [D, TOK])
        xn = sb("xn", [D, TOK])
        sq = sb("sq", [D, 2, CH])
        std = sb("std", [D, 2, CH])
        qT = sb("qT", [D, TOK])
        ctxr = sb("ctxr", [D, 4, S_PAD])
        Ksb = sb("Ksb", [D, 2, S_CTX])
        Vsb = sb("Vsb", [KCH, 2, NCH, D])
        qbd = sb("qbd", [D, 2, HG, T])
        P = sb("P", [128, 2, NG, S_PAD])
        PT = sb("PT", [KCH, NG, NCH, 128])
        nmx = sb("nmx", [128, 2, NG])
        rsum = sb("rsum", [128, 2, NG])
        rinv = sb("rinv", [128, NG])
        mr = sb("mr", [128, NG, HG])
        avm = sb("avm", [128, D])
        rowf = sb("rowf", [128, T, ROWF])
        xs = sb("xs", [D, 2, NB])
        KN = sb("KN", [128, T, G2, N_ST])
        BT = sb("BT", [128, T, G2, N_ST])
        nrm = sb("nrm", [128, T * G2])
        nrm2 = sb("nrm2", [128, T * G2])
        nrm3 = sb("nrm3", [128, T * G2])
        lmax = sb("lmax", [128, T])
        lsh = sb("lsh", [128, T, BLK])
        lexp = sb("lexp", [128, T, BLK])
        lsum = sb("lsum", [128, T])
        linv = sb("linv", [128, T])
        sm = sb("sm", [128, T, BLK])
        cmpa = sb("cmpa", [128, T, BLK, BLK])
        cmpb = sb("cmpb", [128, T, BLK, BLK])
        rank = sb("rank", [128, T, BLK])
        msel = sb("msel", [128, T, BLK])
        usum = sb("usum", [128, T])
        uinv = sb("uinv", [128, T])
        uw = sb("uw", [128, T, BLK])
        wown = sb("wown", [128, T, G2])
        omw = sb("omw", [128, T, G2])
        smo = sb("smo", [128, T, G2])
        S = sb("S", [128, 2, G2, N_ST, N_ST])
        SP = sb("SP", [128, G2, N_ST, N_ST])
        A = sb("A", [128, G2, N_ST, N_ST])
        P1 = sb("P1", [128, G2, N_ST, N_ST])
        QP = sb("QP", [128, 2, G2, N_ST, N_ST])
        bq = sb("bq", [128, 2, 3, N_ST])
        ret = sb("ret", [128, G2, N_ST])
        dlt = sb("dlt", [128, G2, N_ST])
        SQ = sb("SQ", [128, T, G2, N_ST])
        boT = sb("boT", [G2 * N_ST, 2, CH])
        w1s = P[:, :, :, :].rearrange("p a b c -> p (a b c)")[:, 0:2 * F].rearrange("p (a f) -> p a f", a=2)
        w2s = rowf[:, 0:9, :].rearrange("p a b -> p (a b)")[:, 0:2 * FC * D].rearrange("p (a c f) -> p a c f", a=2, c=FC)
        hid = S[:, :, :, :, :].rearrange("p a g i j -> p (a g i j)").rearrange("p (a c f) -> p a c f", a=2, c=FC)
        acc = QP[:, 0, :, :, :].rearrange("p g i j -> p (g i j)").rearrange("p (t d) -> p t d", t=TT)
        res = SP[:, :, :, :].rearrange("p g i j -> p (g i j)")
        elog = sb("elog", [128, TT, E])
        emax = sb("emax", [128, TT])
        eexp = sb("eexp", [128, TT, E])
        esum = sb("esum", [128, TT])
        pmax = sb("pmax", [128, TT])
        eeq = sb("eeq", [128, TT, E])
        ecmp = sb("ecmp", [128, TT, E, E])
        ecnt = sb("ecnt", [128, TT, E])
        gate = sb("gate", [128, TT, E])
        b1s = sb("b1s", [128, 2, FC])
        gateT = A[0:E, :, :, :].rearrange("p g i j -> p (g i j)").rearrange("p (k q) -> p k q", k=TT)

        cst_in, x_in = sem("cst_in"), sem("x_in")
        ctx_in = [sem(f"ctx_in{i}") for i in range(4)]
        pads = sem("pads")
        ln_mean, ln_cent, ln_sq, ln_var, ln_std, ln_rstd, ln_out = (
            sem(n) for n in ("ln_mean", "ln_cent", "ln_sq", "ln_var", "ln_std", "ln_rstd", "ln_out"))
        q_mm, q_sb = sem("q_mm"), sem("q_sb")
        k_mm, k_sb, v_mm, v_sb, qbd_ok = (sem(n) for n in ("k_mm", "k_sb", "v_mm", "v_sb", "qbd_ok"))
        sc_mm, mx_ok, ex_ok, pt_mm = (sem(n) for n in ("sc_mm", "mx_ok", "ex_ok", "pt_mm"))
        pt_even, pt_odd, av_mm, rinv_ok, mr_ok, avm_ok, ot_mm, ot_sb = (
            sem(n) for n in ("pt_even", "pt_odd", "av_mm", "rinv_ok", "mr_ok", "avm_ok", "ot_mm", "ot_sb"))
        wo_mm, x1_ok, in_mm, xp_ok = (sem(n) for n in ("wo_mm", "x1_ok", "in_mm", "xp_ok"))
        xs_ok, row_mm, row_sb = (sem(n) for n in ("xs_ok", "row_mm", "row_sb"))
        link_ok = sem("link_ok")
        prep, prep_sqrt, prep_sig, prep_exp, prep_ok = (
            sem(n) for n in ("prep", "prep_sqrt", "prep_sig", "prep_exp", "prep_ok"))
        knp_ok, p1_ok, ret_ok, dlt_ok, outer_ok, arg_ok, tanh_ok, st_ok = (
            sem(n) for n in ("knp_ok", "p1_ok", "ret_ok", "dlt_ok", "outer_ok", "arg_ok", "tanh_ok", "st_ok"))
        step_in = sem("step_in")
        keep_ok, bs_ok, qp_ok, sq_mm, sq_sb = (sem(n) for n in ("keep_ok", "bs_ok", "qp_ok", "sq_mm", "sq_sb"))
        fin_sig, fin, bo_ok, bt_mm, bt_sb, y_mm, x2_ok = (
            sem(n) for n in ("fin_sig", "fin", "bo_ok", "bt_mm", "bt_sb", "y_mm", "x2_ok"))
        r_mm, rt, rt_exp, gate_ok, gt_mm, gt_sb, b2_mm, acc_init = (
            sem(n) for n in ("r_mm", "rt", "rt_exp", "gate_ok", "gt_mm", "gt_sb", "b2_mm", "acc_init"))
        w_in = [sem(f"w_in{i}") for i in range(2)]
        b1_ok = sem("b1_ok")
        h_mm, h_sb, o_mm, acc_ok, ft_mm, res_ok, stored = (
            sem(n) for n in ("h_mm", "h_sb", "o_mm", "acc_ok", "ft_mm", "res_ok", "stored"))

        def per_group(eng, step, n=NB):
            for b in range(4):
                step(b, b)
            with eng.Fori(1, n // 4 - 1) as i:
                for u in range(4):
                    step(4 * i + u, 4 + u)
            for b in range(n - 4, n):
                step(b, b)

        def cols(c, w=CH):
            return slice(c * w, (c + 1) * w)

        block = ctx.enter_context(nc.Block())

        @block.sync
        def _(sp):
            sp.dma_start(cst[:, :], cst_d).then_inc(cst_in, 16)
            sp.dma_start(x[:, :], xT).then_inc(x_in, 16)

            def load_ctx(b, pos):
                if pos >= 4:
                    sp.wait_ge(v_mm, b - 3)
                sp.dma_start(ctxr[:, pos % 4, :], ctxT[:, bass.ds(b * S_PAD, S_PAD)]).then_inc(ctx_in[pos % 4], 16)

            per_group(sp, load_ctx)
            def load_expert(e, pos):
                if pos == 0:
                    sp.wait_ge(fin, 3)
                if pos >= 2:
                    sp.wait_ge(o_mm, NC * (e - 1))
                u = pos % 2
                sp.dma_start(w1s[:, u, :], w1_d[:, bass.ds(e * F, F)]).then_inc(w_in[u], 16)
                sp.dma_start(w2s[:, u, :, :], w2_d[:, bass.ds(e * FC, FC), :]).then_inc(w_in[u], 16)

            for e in range(2):
                load_expert(e, e)
            with sp.Fori(1, E // 2) as i:
                for u in range(2):
                    load_expert(2 * i + u, 2 + u)
            for c in range(NC):
                sp.wait_ge(res_ok, c + 1)
                sp.dma_start(out_d[:, cols(c)], res[:, cols(c)]).then_inc(stored, 16)
            sp.wait_ge(stored, 16 * NC)

        @block.tensor
        def _(pe):
            mm, tr = nc.tensor.matmul, nc.tensor.transpose

            def layernorm(s, ready):
                def mean(c):
                    n = NC * s + c
                    pe.wait_ge(ready, ready_at(s, c))
                    if c >= 2:
                        pe.wait_ge(ln_cent, n - 1)
                    mm(bank[c % 2][:, :], C("mean"), x[:, cols(c)], start=True, stop=True).then_inc(ln_mean, 1)

                mean(0)
                for c in range(NC):
                    n = NC * s + c
                    if c + 1 < NC:
                        mean(c + 1)
                    pe.wait_ge(ln_sq, n + 1)
                    if c >= 2:
                        pe.wait_ge(ln_std, n - 1)
                    mm(bank[2 + c % 2][:, :], C("mean"), sq[:, c % 2, :], start=True, stop=True).then_inc(ln_var, 1)

            def ready_at(s, c):
                return 16 if s == 0 else c + 1

            pe.wait_ge(cst_in, 16)
            layernorm(0, x_in)
            for c in range(NC):
                pe.wait_ge(ln_out, c + 1)
                if c >= 2:
                    pe.wait_ge(q_sb, c - 1)
                mm(bank[4 + c % 2][:, :], C("wq"), xn[:, cols(c)], start=True, stop=True).then_inc(q_mm, 1)

            def K(b, pos):
                pe.wait_ge(ctx_in[pos % 4], 16 * (b // 4 + 1) if isinstance(b, int) else 4 * (b - pos % 4) + 16)
                if pos >= 1:
                    pe.wait_ge(v_sb, b)
                mm(bank[2][:, 0:S_CTX], C("wk"), ctxr[:, pos % 4, 0:S_CTX], start=True, stop=True).then_inc(k_mm, 1)

            def V(b, pos):
                pe.wait_ge(k_sb, b + 1)
                for c in range(NCH):
                    last = mm(bank[2][0:KCH, c * D:(c + 1) * D], ctxr[:, pos % 4, c * KCH:(c + 1) * KCH], C("wv"),
                              start=True, stop=True)
                last.then_inc(v_mm, 1)

            def scores(b, pos, half):
                if half == 0:
                    pe.wait_ge(k_sb, b + 1)
                    pe.wait_ge(qbd_ok, b + 1)
                if pos >= 1:
                    pe.wait_ge(ex_ok, 2 * b + half - 1)
                for g in (2 * half, 2 * half + 1):
                    r = slice(32 * g, 32 * g + 32)
                    last = mm(bank[4 + g][:, 0:S_CTX], qbd[r, pos % 2, :, :], Ksb[r, pos % 2, :], start=True, stop=True)
                last.then_inc(sc_mm, 1)

            def transposes(b, pos, g):
                pe.wait_ge(ex_ok, 2 * b + g // 2 + 1)
                if pos >= 1 or g >= 2:
                    pe.wait_ge(pt_odd if g % 2 else pt_even, 2 * b + g // 2)
                for c in range(NCH):
                    last = tr(bank[g % 2][0:KCH, c * 128:(c + 1) * 128], P[:, pos % 2, g, c * KCH:(c + 1) * KCH],
                              C("ident"))
                last.then_inc(pt_mm, 1)

            def av(b, pos, g):
                if g == 0:
                    pe.wait_ge(v_sb, b + 1)
                    if pos >= 1:
                        pe.wait_ge(ot_sb, b)
                pe.wait_ge(pt_odd if g % 2 else pt_even, 2 * b + g // 2 + 1)
                for c in range(NCH):
                    last = mm(bank[3][:, 32 * g:32 * g + 32], PT[:, g, c, :], Vsb[:, pos % 2, c, 32 * g:32 * g + 32],
                              start=(c == 0), stop=(c == NCH - 1))
                if g == NG - 1:
                    last.then_inc(av_mm, 1)

            def heads_out(b):
                pe.wait_ge(avm_ok, b + 1)
                mm(bank[3][:, 128:128 + T], avm[:, :], C("sum_heads"), start=True, stop=True).then_inc(ot_mm, 1)

            def row(b, pos):
                if pos < NB - 1:
                    scores(b + 1, pos + 1, 0)
                if pos >= 1:
                    heads_out(b - 1)
                transposes(b, pos, 0)
                transposes(b, pos, 1)
                if pos < NB - 1:
                    scores(b + 1, pos + 1, 1)
                av(b, pos, 0)
                av(b, pos, 1)
                transposes(b, pos, 2)
                transposes(b, pos, 3)
                if pos < NB - 2:
                    K(b + 2, pos + 2)
                av(b, pos, 2)
                av(b, pos, 3)
                if pos < NB - 2:
                    V(b + 2, pos + 2)

            pe.wait_ge(q_sb, NC)
            pe.wait_ge(pads, 2)
            for b in range(2):
                K(b, b)
                V(b, b)
            for half in range(2):
                scores(0, 0, half)
            per_group(pe, row)
            heads_out(NB - 1)
            for c in range(NC):
                pe.wait_ge(ot_sb, NB)
                if c >= 2:
                    pe.wait_ge(x1_ok, c - 1)
                mm(bank[c % 2][:, :], C("wo"), qT[:, cols(c)], start=True, stop=True).then_inc(wo_mm, 1)

            pe.wait_ge(x1_ok, NC)
            layernorm(1, x1_ok)
            for c in range(NC):
                pe.wait_ge(ln_out, NC + c + 1)
                if c >= 2:
                    pe.wait_ge(xp_ok, c - 1)
                mm(bank[4 + c % 2][:, :], C("win"), xn[:, cols(c)], start=True, stop=True).then_inc(in_mm, 1)

            def row_features(t, pos):
                pe.wait_ge(xs_ok, t + 1)
                if pos >= 2:
                    pe.wait_ge(row_sb, t - 1)
                for n2 in range(2):
                    last = mm(bank[pos % 2][64 * n2:64 * n2 + 64, 0:ROWF], xs[:, pos % 2, :], C(f"wrow{n2}"),
                              start=True, stop=True)
                last.then_inc(row_mm, 1)

            for t in range(2):
                row_features(t, t)
            with pe.Fori(1, T // 2) as i:
                for u in range(2):
                    row_features(2 * i + u, 2 + u)

            def readout(t, pos):
                pe.wait_ge(qp_ok, 2 * t + 2)
                if pos >= 2:
                    pe.wait_ge(sq_sb, t - 1)
                for j in range(N_ST):
                    last = mm(bank[2 + pos % 2][:, 0:G2 * N_ST], C("ident"),
                              QP[:, pos % 2, :, :, j].rearrange("p g i -> p (g i)"), start=(j == 0), stop=(j == N_ST - 1))
                last.then_inc(sq_mm, 1)

            for t in range(2):
                readout(t, t)
            with pe.Fori(1, T // 2) as i:
                for u in range(2):
                    readout(2 * i + u, 2 + u)

            pe.wait_ge(bo_ok, 1)
            tb = CH // NB
            for c in range(NC):
                if c >= 2:
                    pe.wait_ge(bt_sb, c - 1)
                for k in range(tb):
                    last = mm(bank[c % 2][0:G2 * N_ST, k * NB:(k + 1) * NB], KN[:, c * tb + k, :, :], C("sum_halves"),
                              start=True, stop=True)
                last.then_inc(bt_mm, 1)
                pe.wait_ge(bt_sb, c + 1)
                if c >= 2:
                    pe.wait_ge(x2_ok, c - 1)
                mm(bank[4 + c % 2][:, :], cst[0:G2 * N_ST, COL["wout"][0]:COL["wout"][1]], boT[:, c % 2, :],
                   start=True, stop=True).then_inc(y_mm, 1)

            pe.wait_ge(x2_ok, NC)
            layernorm(2, x2_ok)
            for k in range(TT):
                pe.wait_ge(ln_out, 2 * NC + k // 4 + 1)
                last = mm(bank[4][:, k * E:(k + 1) * E], xn[:, cols(k, D)], C("wr"), start=True, stop=True)
            last.then_inc(r_mm, 1)
            pe.wait_ge(gate_ok, 1)
            for c in range(NC):
                if c >= 2:
                    pe.wait_ge(gt_sb, c - 1)
                for k in range(4):
                    last = tr(bank[c % 2][0:E, k * 128:(k + 1) * 128], gate[:, 4 * c + k, :], C("ident"))
                last.then_inc(gt_mm, 1)
                pe.wait_ge(gt_sb, c + 1)
                if c >= 2:
                    pe.wait_ge(acc_init, c - 1)
                for k in range(4):
                    last = mm(bank[2 + c % 2][:, k * D:(k + 1) * D], gateT[:, 4 * c + k, :],
                              cst[0:E, COL["b2"][0]:COL["b2"][1]], start=True, stop=True)
                last.then_inc(b2_mm, 1)
            pe.wait_ge(acc_init, NC)

            def expert(e, pos):
                u = pos % 2
                pe.wait_ge(w_in[u], 16 * (e + 2 - u))
                for c in range(NC):
                    n = NC * e + c
                    for f in range(FC):
                        if pos > 0 or c > 0:
                            pe.wait_ge(h_sb, FC * n + f - 3)
                        mm(bank[f][:, :], w1s[:, u, f * D:(f + 1) * D], xn[:, cols(c)],
                           start=True, stop=True).then_inc(h_mm, 1)
                    pe.wait_ge(h_sb, FC * (n + 1))
                    if pos > 0 or c >= 2:
                        pe.wait_ge(acc_ok, n - 1)
                    for k in range(4):
                        for f in range(FC):
                            last = mm(bank[4 + c % 2][:, k * D:(k + 1) * D], hid[:, c % 2, f, k * 128:(k + 1) * 128],
                                      w2s[:, u, f, :], start=(f == 0), stop=(f == FC - 1))
                    last.then_inc(o_mm, 1)

            for e in range(2):
                expert(e, e)
            with pe.Fori(1, E // 2) as i:
                for u in range(2):
                    expert(2 * i + u, 2 + u)
            pe.wait_ge(acc_ok, E * NC)
            for c in range(NC):
                if c >= 2:
                    pe.wait_ge(res_ok, c - 1)
                for k in range(4):
                    last = tr(bank[6 + c % 2][:, k * 128:(k + 1) * 128], acc[:, 4 * c + k, :], C("ident"))
                last.then_inc(ft_mm, 1)

        @block.scalar
        def _(act):
            af = nc.scalar.activation

            def layernorm(s):
                for c in range(NC):
                    n = NC * s + c
                    act.wait_ge(ln_cent, n + 1)
                    if c >= 2:
                        act.wait_ge(ln_var, n - 1)
                    af(sq[:, c % 2, :], xc[:, cols(c)], ACT.Square).then_inc(ln_sq, 1)
                    act.wait_ge(ln_var, n + 1)
                    if c >= 2:
                        act.wait_ge(ln_rstd, n - 1)
                    af(std[:, c % 2, :], bank[2 + c % 2][:, :], ACT.Sqrt, bias=C("eps")).then_inc(ln_std, 1)

            act.wait_ge(cst_in, 16)
            layernorm(0)

            def k_out(b, pos):
                act.wait_ge(k_mm, b + 1)
                if pos >= 2:
                    act.wait_ge(sc_mm, 2 * b - 2)
                af(Ksb[:, pos % 2, :], bank[2][:, 0:S_CTX], ACT.Identity, bias=C("bk")).then_inc(k_sb, 1)

            def exps(b, pos, half):
                act.wait_ge(mx_ok, 2 * b + half + 1)
                if pos >= 2 and half == 0:
                    act.wait_ge(pt_mm, 4 * b - 4)
                    act.wait_ge(avm_ok, b - 1)
                for g in (2 * half, 2 * half + 1):
                    last = af(P[:, pos % 2, g, 0:S_CTX], bank[4 + g][:, 0:S_CTX], ACT.Exp,
                              bias=nmx[:, pos % 2, g:g + 1], accum_out=rsum[:, pos % 2, g:g + 1])
                last.then_inc(ex_ok, 1)

            def pt_out(b, g):
                act.wait_ge(pt_mm, 4 * b + g + 1)
                nc.scalar.copy(PT[:, g, :, :].rearrange("k c q -> k (c q)"), bank[1][0:KCH, 0:NCH * 128]).then_inc(pt_odd, 1)

            def row(b, pos):
                if pos < NB - 1:
                    exps(b + 1, pos + 1, 0)
                pt_out(b, 1)
                if pos < NB - 1:
                    exps(b + 1, pos + 1, 1)
                pt_out(b, 3)
                if pos < NB - 2:
                    k_out(b + 2, pos + 2)

            act.wait_ge(pads, 2)
            act.wait_ge(q_sb, NC)
            for b in range(2):
                k_out(b, b)
            for half in range(2):
                exps(0, 0, half)
            per_group(act, row)

            layernorm(1)
            for c in range(NC):
                act.wait_ge(in_mm, c + 1)
                af(qT[:, cols(c)], bank[4 + c % 2][:, :], ACT.Silu).then_inc(xp_ok, 1)

            def step_tokens(t, pos):
                if pos >= 2:
                    act.wait_ge(row_mm, t - 1)
                nc.scalar.copy(xs[:, pos % 2, :], qT[:, bass.ds(t * NB, NB)]).then_inc(xs_ok, 1)

            act.wait_ge(xp_ok, NC)
            for t in range(2):
                step_tokens(t, t)
            with act.Fori(1, T // 2) as i:
                for u in range(2):
                    step_tokens(2 * i + u, 2 + u)

            act.wait_ge(prep, 3)
            af(nrm2[:, :], nrm[:, :], ACT.Sqrt).then_inc(prep_sqrt, 1)
            af(lexp[:, :, :], lsh[:, :, :], ACT.Exp).then_inc(prep_exp, 1)
            af(BT[:, :, :, :], BT[:, :, :, :], ACT.Sigmoid).then_inc(prep_sig, 1)

            def sq_out(t, pos):
                act.wait_ge(sq_mm, t + 1)
                nc.scalar.copy(SQ[:, bass.ds(t, 1), :, :].rearrange("p o g i -> p (o g i)"),
                               bank[2 + pos % 2][:, 0:G2 * N_ST]).then_inc(sq_sb, 1)

            def beta_query(t, pos):
                if pos >= 2:
                    act.wait_ge(qp_ok, 2 * t - 2)
                nc.scalar.copy(bq[:, pos % 2, 0:2, :], BT[:, bass.ds(t, 1), :, :].rearrange("p o g i -> p (o g) i")).then_inc(step_in, 1)
                nc.scalar.copy(bq[:, pos % 2, 2:3, :], rowf[:, bass.ds(t, 1), 192:224]).then_inc(step_in, 1)

            def step(t, pos):
                for g in range(G2):
                    act.wait_ge(st_ok, 2 * t + g + 1)
                    af(SP[:, g, :, :], S[:, pos % 2, g, :, :], ACT.Copy,
                       scale=omw[:, bass.ds(t, 1), g]).then_inc(keep_ok, 1)
                for g in range(G2):
                    act.wait_ge(arg_ok, 2 * t + g + 1)
                    ps = pair[g][:, :, :].rearrange("p a f -> p (a f)")
                    af(ps, ps, ACT.Tanh).then_inc(tanh_ok, 1)
                if pos < T - 1:
                    beta_query(t + 1, pos + 1)
                if pos >= 1:
                    sq_out(t - 1, pos - 1)

            act.wait_ge(prep_ok, 1)
            act.wait_ge(prep_sig, 1)
            beta_query(0, 0)
            for t in range(2):
                step(t, t)
            with act.Fori(1, T // 2 - 1) as i:
                for u in range(2):
                    step(2 * i + u, 2 + u)
            for t in range(T - 2, T):
                step(t, t)
            sq_out(T - 1, T - 1)
            act.wait_ge(sq_sb, T)
            af(BT[:, :, :, :], SQ[:, :, :, :], ACT.Sigmoid).then_inc(fin_sig, 1)
            for c in range(NC):
                act.wait_ge(bt_mm, c + 1)
                if c >= 2:
                    act.wait_ge(y_mm, c - 1)
                nc.scalar.copy(boT[:, c % 2, :], bank[c % 2][0:G2 * N_ST, :]).then_inc(bt_sb, 1)

            layernorm(2)
            act.wait_ge(rt, 2)
            af(eexp[:, :, :], elog[:, :, :], ACT.Exp).then_inc(rt_exp, 1)

            def expert(e, pos):
                nc.scalar.copy(b1s[:, pos % 2, :], cst[:, bass.ds(e * FC + COL["b1"][0], FC)]).then_inc(b1_ok, 1)
                act.wait_ge(b1_ok, e + 1)
                for c in range(NC):
                    n = NC * e + c
                    if pos > 0 or c >= 2:
                        act.wait_ge(o_mm, n - 1)
                    for f in range(FC):
                        act.wait_ge(h_mm, FC * n + f + 1)
                        af(hid[:, c % 2, f, :], bank[f][:, :], ACT.Gelu,
                           bias=b1s[:, pos % 2, f:f + 1]).then_inc(h_sb, 1)

            for e in range(2):
                expert(e, e)
            with act.Fori(1, E // 2) as i:
                for u in range(2):
                    expert(2 * i + u, 2 + u)

        @block.gpsimd
        def _(pool):
            pool.memset(P[:, :, :, S_CTX:S_PAD], 0.0).then_inc(pads, 1)
            pool.memset(S[:, 0, :, :, :], 0.0).then_inc(pads, 1)
            pool.wait_ge(cst_in, 16)
            pool.wait_ge(q_sb, NC)
            q_tb = qT[:, :].rearrange("p (t b) -> p b t", b=NB)

            def blockdiag(b, pos):
                if pos >= 2:
                    pool.wait_ge(sc_mm, 2 * b - 2)
                pool.tensor_tensor(qbd[:, pos % 2, :, :],
                                   q_tb[:, bass.ds(b, 1), :].to_broadcast([D, HG, T]),
                                   C("head_of_row").unsqueeze(2).to_broadcast([D, HG, T]), ALU.mult).then_inc(qbd_ok, 1)

            per_group(pool, blockdiag)
            pool.wait_ge(prep_ok, 1)

            def beta_state(t, pos):
                pool.wait_ge(step_in, 2 * t + 2)
                for g in range(G2):
                    pool.wait_ge(st_ok, 2 * t + g + 1)
                    if pos >= 1:
                        pool.wait_ge(arg_ok, 2 * t + g - 1)
                    pool.tensor_tensor(A[:, g, :, :], S[:, pos % 2, g, :, :],
                                       bq[:, pos % 2, g, :].unsqueeze(2).to_broadcast([128, N_ST, N_ST]),
                                       ALU.mult).then_inc(bs_ok, 1)

            def query_state(t, pos):
                for g in range(G2):
                    pool.wait_ge(st_ok, 2 * t + g + 3)
                    if pos >= 2 and g == 0:
                        pool.wait_ge(sq_mm, t - 1)
                    pool.tensor_tensor(QP[:, pos % 2, g, :, :], S[:, (pos + 1) % 2, g, :, :],
                                       bq[:, pos % 2, 2:3, :].to_broadcast([128, N_ST, N_ST]),
                                       ALU.mult).then_inc(qp_ok, 1)

            def step(t, pos):
                if pos < T - 1:
                    beta_state(t + 1, pos + 1)
                query_state(t, pos)

            beta_state(0, 0)
            for t in range(2):
                step(t, t)
            with pool.Fori(1, T // 2 - 1) as i:
                for u in range(2):
                    step(2 * i + u, 2 + u)
            for t in range(T - 2, T):
                step(t, t)

        @block.vector
        def _(dve):
            v = nc.vector

            def layernorm(s):
                def centre(c):
                    dve.wait_ge(ln_mean, NC * s + c + 1)
                    v.tensor_tensor(xc[:, cols(c)], x[:, cols(c)], bank[c % 2][:, :], ALU.subtract).then_inc(ln_cent, 1)

                centre(0)
                for c in range(NC):
                    n = NC * s + c
                    if c + 1 < NC:
                        centre(c + 1)
                    dve.wait_ge(ln_std, n + 1)
                    v.reciprocal(std[:, c % 2, :], std[:, c % 2, :]).then_inc(ln_rstd, 1)
                    dve.wait_ge(ln_rstd, n + 1)
                    v.tensor_tensor(xn[:, cols(c)], xc[:, cols(c)], std[:, c % 2, :], ALU.mult).then_inc(ln_out, 1)

            dve.wait_ge(cst_in, 16)
            dve.wait_ge(x_in, 16)
            layernorm(0)
            for c in range(NC):
                dve.wait_ge(q_mm, c + 1)
                v.tensor_scalar(qT[:, cols(c)], bank[4 + c % 2][:, :], C("bq"), DH ** -0.5, ALU.add, ALU.mult).then_inc(q_sb, 1)

            def v_out(b, pos):
                dve.wait_ge(v_mm, b + 1)
                v.tensor_copy(Vsb[:, pos % 2, :, :].rearrange("k c d -> k (c d)"), bank[2][0:KCH, 0:NCH * D]).then_inc(v_sb, 1)

            def maxes(b, pos, half):
                dve.wait_ge(sc_mm, 2 * b + half + 1)
                v.tensor_reduce(nmx[:, pos % 2, 2 * half:2 * half + 2], pair[half][:, :, 0:S_CTX], AX.X, ALU.max,
                                negate=True).then_inc(mx_ok, 1)

            def pt_out(b, g):
                dve.wait_ge(pt_mm, 4 * b + g + 1)
                v.tensor_copy(PT[:, g, :, :].rearrange("k c q -> k (c q)"), bank[0][0:KCH, 0:NCH * 128]).then_inc(pt_even, 1)

            def own_heads(b, pos):
                dve.wait_ge(ex_ok, 2 * b + 2)
                v.reciprocal(rinv[:, :], rsum[:, pos % 2, :]).then_inc(rinv_ok, 1)
                dve.wait_ge(rinv_ok, b + 1)
                v.tensor_tensor(mr[:, :, :], rinv[:, :].unsqueeze(2).to_broadcast([128, NG, HG]),
                                C("own_head").unsqueeze(1).to_broadcast([128, NG, HG]), ALU.mult).then_inc(mr_ok, 1)
                dve.wait_ge(mr_ok, b + 1)
                dve.wait_ge(av_mm, b + 1)
                if pos >= 1:
                    dve.wait_ge(ot_mm, b)
                v.tensor_tensor(avm[:, :].rearrange("p (h d) -> p h d", d=DH),
                                bank[3][:, 0:D].rearrange("p (h d) -> p h d", d=DH),
                                mr[:, :, :].rearrange("p g h -> p (g h)").unsqueeze(2).to_broadcast([128, H, DH]),
                                ALU.mult).then_inc(avm_ok, 1)

            o_tb = qT[:, :].rearrange("p (t b) -> p b t", b=NB)

            def heads_out(b):
                dve.wait_ge(ot_mm, b + 1)
                dve.wait_ge(qbd_ok, b + 1)
                v.tensor_scalar(o_tb[:, bass.ds(b, 1), :].rearrange("p o t -> p (o t)"), bank[3][:, 128:128 + T], C("bv"), None,
                                ALU.add).then_inc(ot_sb, 1)

            def row(b, pos):
                if pos < NB - 1:
                    maxes(b + 1, pos + 1, 0)
                if pos >= 1:
                    heads_out(b - 1)
                pt_out(b, 0)
                if pos < NB - 1:
                    maxes(b + 1, pos + 1, 1)
                pt_out(b, 2)
                own_heads(b, pos)
                if pos < NB - 2:
                    v_out(b + 2, pos + 2)

            for b in range(2):
                v_out(b, b)
            for half in range(2):
                maxes(0, 0, half)
            per_group(dve, row)
            heads_out(NB - 1)
            for c in range(NC):
                dve.wait_ge(wo_mm, c + 1)
                v.scalar_tensor_tensor(x[:, cols(c)], bank[c % 2][:, :], C("bo"), x[:, cols(c)], ALU.add,
                                       ALU.add).then_inc(x1_ok, 1)

            layernorm(1)

            def row_out(t, pos):
                dve.wait_ge(row_mm, t + 1)
                v.tensor_copy(rowf[:, bass.ds(t, 1), :].rearrange("p o f -> p (o f)"), bank[pos % 2][:, 0:ROWF]).then_inc(row_sb, 1)

            for t in range(2):
                row_out(t, t)
            with dve.Fori(1, T // 2) as i:
                for u in range(2):
                    row_out(2 * i + u, 2 + u)

            chain = [0]

            def link(ins):
                chain[0] += 1
                ins.then_inc(link_ok, 1)
                dve.wait_ge(link_ok, chain[0])

            dve.wait_ge(row_sb, T)
            kraw = rowf[:, :, 0:64].rearrange("p t (g j) -> p t g j", g=G2)
            logit = rowf[:, :, 224:228]
            link(v.tensor_tensor(KN[:, :, :, :], kraw, kraw, ALU.mult))
            v.tensor_reduce(nrm[:, :], KN[:, :, :, :].rearrange("p t g j -> p (t g) j"), AX.X, ALU.add).then_inc(prep, 1)
            v.tensor_tensor(BT[:, :, :, :].rearrange("p t g i -> p t (g i)"), rowf[:, :, 128:192],
                            C("bbeta").unsqueeze(1).to_broadcast([128, T, G2 * N_ST]), ALU.add).then_inc(prep, 1)
            link(v.tensor_reduce(lmax[:, :], logit, AX.X, ALU.max))
            v.tensor_tensor(lsh[:, :, :], logit, lmax[:, :].unsqueeze(2).to_broadcast([128, T, BLK]),
                            ALU.subtract).then_inc(prep, 1)
            lm = logit.unsqueeze(2).to_broadcast([128, T, BLK, BLK])
            ln = logit.unsqueeze(3).to_broadcast([128, T, BLK, BLK])

            def tri(name):
                return C(name).rearrange("p (n m) -> p n m", m=BLK).unsqueeze(1).to_broadcast([128, T, BLK, BLK])

            v.tensor_tensor(cmpa[:, :, :, :], lm, ln, ALU.is_ge).then_inc(link_ok, 1)
            v.tensor_tensor(cmpb[:, :, :, :], lm, ln, ALU.is_gt).then_inc(link_ok, 1)
            chain[0] += 2
            dve.wait_ge(link_ok, chain[0])
            v.tensor_tensor(cmpa[:, :, :, :], cmpa[:, :, :, :], tri("low4"), ALU.mult).then_inc(link_ok, 1)
            v.tensor_tensor(cmpb[:, :, :, :], cmpb[:, :, :, :], tri("up4"), ALU.mult).then_inc(link_ok, 1)
            chain[0] += 2
            dve.wait_ge(link_ok, chain[0])
            link(v.tensor_tensor(cmpa[:, :, :, :], cmpa[:, :, :, :], cmpb[:, :, :, :], ALU.add))
            link(v.tensor_reduce(rank[:, :, :], cmpa[:, :, :, :], AX.X, ALU.add))
            link(v.tensor_scalar(msel[:, :, :], rank[:, :, :], 2.0, None, ALU.is_lt))
            dve.wait_ge(prep_exp, 1)
            link(v.tensor_reduce(lsum[:, :], lexp[:, :, :], AX.X, ALU.add))
            link(v.reciprocal(linv[:, :], lsum[:, :]))
            link(v.tensor_tensor(sm[:, :, :], lexp[:, :, :], linv[:, :].unsqueeze(2).to_broadcast([128, T, BLK]), ALU.mult))
            link(v.tensor_tensor(msel[:, :, :], msel[:, :, :], sm[:, :, :], ALU.mult))
            link(v.tensor_reduce(usum[:, :], msel[:, :, :], AX.X, ALU.add))
            link(v.tensor_scalar(usum[:, :], usum[:, :], 1e-8, None, ALU.add))
            link(v.reciprocal(uinv[:, :], usum[:, :]))
            link(v.tensor_tensor(uw[:, :, :], msel[:, :, :], uinv[:, :].unsqueeze(2).to_broadcast([128, T, BLK]), ALU.mult))
            for n2 in range(2):
                half = slice(64 * n2, 64 * n2 + 64)
                link(v.tensor_copy(wown[half, :, :], uw[half, :, n2::2]))
                link(v.tensor_copy(smo[half, :, :], sm[half, :, n2::2]))
            link(v.tensor_scalar(omw[:, :, :], wown[:, :, :], -1.0, 1.0, ALU.mult, ALU.add))
            dve.wait_ge(prep_sqrt, 1)
            link(v.tensor_scalar(nrm3[:, :], nrm2[:, :], 1e-6, None, ALU.add))
            link(v.reciprocal(nrm3[:, :], nrm3[:, :]))
            link(v.tensor_tensor(KN[:, :, :, :], kraw,
                                 nrm3[:, :].rearrange("p (t g) -> p t g", g=G2).unsqueeze(3).to_broadcast([128, T, G2, N_ST]),
                                 ALU.mult))
            dve.wait_ge(prep_sig, 1)
            dve.wait_ge(pads, 2)
            v.tensor_copy(nrm2[:, 0:1], nrm3[:, 0:1]).then_inc(prep_ok, 1)
            for g in range(G2):
                v.tensor_copy(nrm[:, g:g + 1], nrm3[:, g:g + 1]).then_inc(st_ok, 1)

            knp = [bank[0], bank[1]]

            def step(t, pos):
                pp = pos % 2
                kn = knp[pp][:, 0:G2 * N_ST]
                v.tensor_copy(kn, KN[:, bass.ds(t, 1), :, :].rearrange("p o g j -> p (o g j)")).then_inc(knp_ok, 1)
                dve.wait_ge(knp_ok, t + 1)
                for g in range(G2):
                    knb = kn[:, g * N_ST:(g + 1) * N_ST].unsqueeze(1).to_broadcast([128, N_ST, N_ST])
                    psg = pair[g][:, :, :].rearrange("p a (i j) -> p (a i) j", j=N_ST)
                    n = 2 * t + g + 1
                    dve.wait_ge(st_ok, n)
                    v.tensor_tensor(P1[:, g, :, :], S[:, pp, g, :, :], knb, ALU.mult).then_inc(p1_ok, 1)
                    dve.wait_ge(p1_ok, n)
                    v.tensor_reduce(ret[:, g, :], P1[:, g, :, :], AX.X, ALU.add).then_inc(ret_ok, 1)
                    dve.wait_ge(ret_ok, n)
                    v.tensor_tensor(dlt[:, g, :], rowf[:, bass.ds(t, 1), 64 + 32 * g:96 + 32 * g].rearrange("p o i -> p (o i)"),
                                    ret[:, g, :], ALU.subtract).then_inc(dlt_ok, 1)
                    dve.wait_ge(dlt_ok, n)
                    v.tensor_tensor(psg, dlt[:, g, :].unsqueeze(2).to_broadcast([128, N_ST, N_ST]), knb,
                                    ALU.mult).then_inc(outer_ok, 1)
                    dve.wait_ge(outer_ok, n)
                    dve.wait_ge(bs_ok, n)
                    v.tensor_tensor(psg, psg, A[:, g, :, :], ALU.add).then_inc(arg_ok, 1)
                for g in range(G2):
                    n = 2 * t + g + 1
                    psg = pair[g][:, :, :].rearrange("p a f -> p (a f)")
                    dve.wait_ge(tanh_ok, n)
                    dve.wait_ge(keep_ok, n)
                    if pos >= 1:
                        dve.wait_ge(qp_ok, n - 2)
                    v.scalar_tensor_tensor(S[:, 1 - pp, g, :, :].rearrange("p i j -> p (i j)"), psg, wown[:, bass.ds(t, 1), g],
                                           SP[:, g, :, :].rearrange("p i j -> p (i j)"), ALU.mult, ALU.add).then_inc(st_ok, 1)

            for t in range(2):
                step(t, t)
            with dve.Fori(1, T // 2) as i:
                for u in range(2):
                    step(2 * i + u, 2 + u)

            dve.wait_ge(sq_sb, T)
            v.tensor_tensor(KN[:, :, :, :], SQ[:, :, :, :], SQ[:, :, :, :], ALU.mult).then_inc(fin, 1)
            dve.wait_ge(fin, 1)
            dve.wait_ge(fin_sig, 1)
            v.tensor_tensor(KN[:, :, :, :], KN[:, :, :, :], BT[:, :, :, :], ALU.mult).then_inc(fin, 1)
            dve.wait_ge(fin, 2)
            v.tensor_tensor(KN[:, :, :, :], KN[:, :, :, :], smo[:, :, :].unsqueeze(3).to_broadcast([128, T, G2, N_ST]),
                            ALU.mult).then_inc(bo_ok, 1)
            dve.wait_ge(bo_ok, 1)
            v.tensor_copy(nrm[:, 0:1], nrm3[:, 0:1]).then_inc(fin, 1)
            for c in range(NC):
                dve.wait_ge(y_mm, c + 1)
                v.tensor_tensor(x[:, cols(c)], x[:, cols(c)], bank[4 + c % 2][:, :], ALU.add).then_inc(x2_ok, 1)

            layernorm(2)
            dve.wait_ge(r_mm, 1)
            lg = bank[4][:, 0:TT * E].rearrange("p (t e) -> p t e", e=E)
            link(v.tensor_reduce(emax[:, :], lg, AX.X, ALU.max))
            v.tensor_tensor(eeq[:, :, :], lg, emax[:, :].unsqueeze(2).to_broadcast([128, TT, E]), ALU.is_ge).then_inc(rt, 1)
            v.tensor_tensor(elog[:, :, :], lg, emax[:, :].unsqueeze(2).to_broadcast([128, TT, E]), ALU.subtract).then_inc(rt, 1)
            dve.wait_ge(rt, 2)
            link(v.tensor_tensor(ecmp[:, :, :, :], eeq[:, :, :].unsqueeze(2).to_broadcast([128, TT, E, E]),
                                 C("low8").rearrange("p (n m) -> p n m", m=E).unsqueeze(1).to_broadcast([128, TT, E, E]),
                                 ALU.mult))
            link(v.tensor_reduce(ecnt[:, :, :], ecmp[:, :, :, :], AX.X, ALU.add))
            link(v.tensor_scalar(ecnt[:, :, :], ecnt[:, :, :], 1.0, None, ALU.is_lt))
            link(v.tensor_tensor(eeq[:, :, :], eeq[:, :, :], ecnt[:, :, :], ALU.mult))
            dve.wait_ge(rt_exp, 1)
            link(v.tensor_reduce(esum[:, :], eexp[:, :, :], AX.X, ALU.add))
            link(v.reciprocal(pmax[:, :], esum[:, :]))
            v.tensor_tensor(gate[:, :, :], eeq[:, :, :], pmax[:, :].unsqueeze(2).to_broadcast([128, TT, E]),
                            ALU.mult).then_inc(gate_ok, 1)
            dve.wait_ge(gate_ok, 1)
            for c in range(NC):
                dve.wait_ge(gt_mm, c + 1)
                v.tensor_copy(gateT[:, 4 * c:4 * c + 4, :].rearrange("e k q -> e (k q)"), bank[c % 2][0:E, :]).then_inc(gt_sb, 1)
                dve.wait_ge(b2_mm, c + 1)
                v.tensor_copy(acc[:, 4 * c:4 * c + 4, :].rearrange("p k d -> p (k d)"), bank[2 + c % 2][:, :]).then_inc(acc_init, 1)
            dve.wait_ge(acc_init, NC)

            def expert(e, pos):
                for c in range(NC):
                    n = NC * e + c
                    dve.wait_ge(o_mm, n + 1)
                    if pos > 0:
                        dve.wait_ge(acc_ok, n - (NC - 1))
                    for k in range(4):
                        last = v.scalar_tensor_tensor(acc[:, 4 * c + k, :], bank[4 + c % 2][:, k * D:(k + 1) * D],
                                                      gate[:, 4 * c + k, bass.ds(e, 1)], acc[:, 4 * c + k, :],
                                                      ALU.mult, ALU.add)
                    last.then_inc(acc_ok, 1)

            for e in range(2):
                expert(e, e)
            with dve.Fori(1, E // 2) as i:
                for u in range(2):
                    expert(2 * i + u, 2 + u)
            for c in range(NC):
                dve.wait_ge(ft_mm, c + 1)
                v.tensor_tensor(res[:, cols(c)], x[:, cols(c)], bank[6 + c % 2][:, :], ALU.add).then_inc(res_ok, 1)


def kernel(x, ctx_1024, L0_xattn_Wq, L0_xattn_bq, L0_xattn_Wk, L0_xattn_bk, L0_xattn_Wv, L0_xattn_bv, L0_xattn_Wo,
           L0_xattn_bo, L0_attn_W_in, L0_attn_W_router, L0_attn_W_kv, L0_attn_W_beta, L0_attn_b_beta, L0_attn_W_q,
           L0_attn_W_out, L0_ffn_Wr, L0_ffn_W1, L0_ffn_b1, L0_ffn_W2, L0_ffn_b2):
    import concourse.bacc as bacc
    from concourse.bass_utils import run_bass_kernel_spmd

    f = np.float32
    n = np.asarray
    xT = n(x).transpose(2, 1, 0).reshape(D, TOK)
    ctxT = np.zeros((D, NB, S_PAD), f)
    ctxT[:, :, :S_CTX] = n(ctx_1024).transpose(2, 0, 1)
    kv = n(L0_attn_W_kv).reshape(BLK, 2, N_ST, D)
    beta = n(L0_attn_W_beta).reshape(BLK, N_ST, D)
    c = np.zeros((128, NCONST), f)

    def put(name, a):
        c[:a.shape[0], COL[name][0]:COL[name][1]] = a

    put("wq", n(L0_xattn_Wq).T)
    put("wk", n(L0_xattn_Wk).T)
    put("wv", n(L0_xattn_Wv).T)
    put("wo", n(L0_xattn_Wo).T)
    put("win", n(L0_attn_W_in).T)
    for h in range(2):
        rows = [kv[h, 0], kv[h + 2, 0], kv[h, 1], kv[h + 2, 1], beta[h], beta[h + 2], n(L0_attn_W_q), n(L0_attn_W_router)]
        put(f"wrow{h}", np.concatenate(rows, 0).T)
    put("wr", n(L0_ffn_Wr))
    p = np.arange(128)
    put("ident", np.eye(128, dtype=f))
    put("mean", np.full((128, 128), 1.0 / D, f))
    put("head_of_row", (p[:, None] // DH % HG == np.arange(HG)).astype(f))
    put("own_head", (p[:, None] // T == np.arange(HG)).astype(f))
    put("sum_heads", (p[:, None] % T == np.arange(T)).astype(f))
    put("sum_halves", (p[:, None] % NB == np.arange(NB)).astype(f))
    put("bq", n(L0_xattn_bq)[:, None])
    put("bk", n(L0_xattn_bk)[:, None])
    put("bv", n(L0_xattn_bv)[:, None])
    put("bo", n(L0_xattn_bo)[:, None])
    bb = n(L0_attn_b_beta)
    put("bbeta", np.repeat(np.stack([np.concatenate([bb[0], bb[2]]), np.concatenate([bb[1], bb[3]])]), NB, 0))
    put("wout", np.tile(n(L0_attn_W_out).T, (G2, 1)))
    put("low4", np.tile(np.tril(np.ones((4, 4), f), -1).reshape(1, 16), (128, 1)))
    put("up4", np.tile(np.triu(np.ones((4, 4), f), 1).reshape(1, 16), (128, 1)))
    put("low8", np.tile(np.tril(np.ones((8, 8), f), -1).reshape(1, 64), (128, 1)))
    put("b1", n(L0_ffn_b1).reshape(E * FC, D).T)
    put("b2", n(L0_ffn_b2))
    put("eps", np.full((128, 1), 1e-5, f))
    w1 = n(L0_ffn_W1).transpose(1, 0, 2).reshape(D, E * F)
    w2 = n(L0_ffn_W2).reshape(E, FC, D, D).transpose(2, 0, 1, 3).reshape(D, E * FC, D)

    nc = bacc.Bacc("TRN2", target_bir_lowering=False, num_devices=1)
    arrays, args = {}, []
    for name, a in [("xT", xT), ("ctxT", ctxT.reshape(D, NB * S_PAD)), ("cst", c), ("w1", w1), ("w2", w2)]:
        a = np.ascontiguousarray(a)
        arrays[f"in_{name}_dram"] = a
        args.append(nc.dram_tensor(f"in_{name}_dram", a.shape, mybir.dt.from_np(a.dtype), kind="ExternalInput").ap())
    args.append(nc.dram_tensor("out_dram", (D, TOK), mybir.dt.float32, kind="ExternalOutput").ap())
    build(nc, *args)
    r = run_bass_kernel_spmd(nc, [arrays], core_ids=[0])
    return np.ascontiguousarray(r.results[0]["out_dram"].reshape(D, T, NB).transpose(2, 1, 0))
```

```python
from contextlib import ExitStack

import numpy as np

import concourse.bass as bass
from concourse import mybir

NB = 64
T = 32
D = 128
TOK = NB * T
S_CTX = 257
KCH = 86
NCH = 3
S_PAD = KCH * NCH
H = 16
DH = D // H
HG = 4
NG = H // HG
N_ST = 32
BLK = 4
G2 = 2
ST = N_ST * N_ST
ROWF = 2 * N_ST * 3 + N_ST + BLK
E = 8
F = 512
FC = F // D
CH = 512
NC = TOK // CH
TT = TOK // D

_COLS = [("wq", D), ("wk", D), ("wv", D), ("wo", D), ("win", D), ("wrow0", ROWF), ("wrow1", ROWF), ("wr", E),
         ("ident", D), ("mean", D), ("head_of_row", HG), ("own_head", HG), ("sum_heads", T), ("sum_halves", NB),
         ("bq", 1), ("bk", 1), ("bv", 1), ("bo", 1), ("bbeta", G2 * N_ST), ("wout", D), ("low4", 16), ("up4", 16),
         ("low8", 64), ("b1", E * FC), ("b2", D), ("eps", 1)]
COL, _at = {}, 0
for _n, _w in _COLS:
    COL[_n] = (_at, _at + _w)
    _at += _w
NCONST = _at


def build(nc, xT, ctxT, cst_d, w1_d, w2_d, out_d):
    fp32 = mybir.dt.float32
    ALU = mybir.AluOpType
    ACT = mybir.ActivationFunctionType
    AX = mybir.AxisListType

    with ExitStack() as ctx:
        def sb(name, shape):
            return ctx.enter_context(nc.sbuf_tensor(name, shape, fp32))

        def sem(name):
            return ctx.enter_context(nc.semaphore(name))

        bank = [ctx.enter_context(nc.psum_tensor(f"bank{i}", [128, 512], fp32)) for i in range(4)]
        pair = [ctx.enter_context(nc.psum_tensor(f"pair{i}", [128, 2, 512], fp32)) for i in range(2)]
        bank += [pair[0][:, 0, :], pair[0][:, 1, :], pair[1][:, 0, :], pair[1][:, 1, :]]

        cst = sb("cst", [128, NCONST])

        def C(name):
            return cst[:, COL[name][0]:COL[name][1]]

        x = sb("x", [D, TOK])
        xcn = sb("xcn", [D, 2, TOK])
        xc, xn = xcn[:, 0, :], xcn[:, 1, :]
        sq = sb("sq", [D, 2, CH])
        std = sb("std", [D, 2, CH])
        qT = sb("qT", [D, TOK])
        ctxr = sb("ctxr", [D, 4, S_PAD])
        Ksb = sb("Ksb", [D, 2, S_CTX])
        Vsb = sb("Vsb", [KCH, 4, NCH, D])
        qbd = sb("qbd", [D, 2, HG, T])
        P = sb("P", [128, 2, NG, S_PAD])
        PT = sb("PT", [KCH, NG, NCH, 128])
        nmx = sb("nmx", [128, 2, NG])
        rsum = sb("rsum", [128, 2, NG])
        rinv = sb("rinv", [128, NG])
        avm = sb("avm", [128, 512])
        osum = sb("osum", [128, 4, T])
        rowf = sb("rowf", [128, T, ROWF])
        xs = sb("xs", [D, 2, NB])
        KN = sb("KN", [128, T, G2, N_ST])
        BT = sb("BT", [128, T, G2, N_ST])
        nrm = sb("nrm", [128, T * G2])
        nrm2 = sb("nrm2", [128, T * G2])
        nrm3 = sb("nrm3", [128, T * G2])
        lmax = sb("lmax", [128, T])
        lsh = sb("lsh", [128, T, BLK])
        lexp = sb("lexp", [128, T, BLK])
        lsum = sb("lsum", [128, T])
        linv = sb("linv", [128, T])
        sm = sb("sm", [128, T, BLK])
        cmpa = sb("cmpa", [128, T, BLK, BLK])
        cmpb = sb("cmpb", [128, T, BLK, BLK])
        rank = sb("rank", [128, T, BLK])
        msel = sb("msel", [128, T, BLK])
        usum = sb("usum", [128, T])
        uinv = sb("uinv", [128, T])
        uw = sb("uw", [128, T, BLK])
        wown = sb("wown", [128, T, G2])
        omw = sb("omw", [128, T, G2])
        smo = sb("smo", [128, T, G2])
        S = sb("S", [128, 2, G2, N_ST, N_ST])
        SP = sb("SP", [128, G2, N_ST, N_ST])
        A = sb("A", [128, G2, N_ST, N_ST])
        P1 = sb("P1", [128, G2, N_ST, N_ST])
        QP = sb("QP", [128, 2, G2, N_ST, N_ST])
        now = sb("now", [128, 2, 5, N_ST])
        ret = sb("ret", [128, G2, N_ST])
        dlt = sb("dlt", [128, G2, N_ST])
        SQ = P1[:, :, :, :].rearrange("p g i j -> p (g i j)").rearrange("p (t g i) -> p t g i", t=T, g=G2)
        SQ2 = xcn[:, :, :].rearrange("p k (t x) -> p k t x", t=T)
        boT = sb("boT", [G2 * N_ST, 2, CH])
        w1s = P[:, :, :, :].rearrange("p a b c -> p (a b c)")[:, 0:2 * F].rearrange("p (a f) -> p a f", a=2)
        w2s = rowf[:, 0:9, :].rearrange("p a b -> p (a b)")[:, 0:2 * FC * D].rearrange("p (a c f) -> p a c f", a=2, c=FC)
        hid = S[:, :, :, :, :].rearrange("p a g i j -> p (a g i j)").rearrange("p (a c f) -> p a c f", a=2, c=FC)
        acc = QP[:, 0, :, :, :].rearrange("p g i j -> p (g i j)").rearrange("p (t d) -> p t d", t=TT)
        res = SP[:, :, :, :].rearrange("p g i j -> p (g i j)")
        elog = sb("elog", [128, TT, E])
        emax = sb("emax", [128, TT])
        eexp = sb("eexp", [128, TT, E])
        esum = sb("esum", [128, TT])
        pmax = sb("pmax", [128, TT])
        eeq = sb("eeq", [128, TT, E])
        ecmp = sb("ecmp", [128, TT, E, E])
        ecnt = sb("ecnt", [128, TT, E])
        gate = sb("gate", [128, TT, E])
        b1s = sb("b1s", [128, 2, FC])
        gateT = A[0:E, :, :, :].rearrange("p g i j -> p (g i j)").rearrange("p (k q) -> p k q", k=TT)

        cst_in, x_in = sem("cst_in"), sem("x_in")
        ctx_in = [sem(f"ctx_in{i}") for i in range(4)]
        pads = sem("pads")
        ln_mean, ln_cent, ln_sq, ln_var, ln_std, ln_rstd, ln_out = (
            sem(n) for n in ("ln_mean", "ln_cent", "ln_sq", "ln_var", "ln_std", "ln_rstd", "ln_out"))
        q_mm, q_sb = sem("q_mm"), sem("q_sb")
        k_mm, k_sb, v_mm, v_sb, qbd_ok = (sem(n) for n in ("k_mm", "k_sb", "v_mm", "v_sb", "qbd_ok"))
        sc_mm, mx_ok, ex_ok, pt_mm = (sem(n) for n in ("sc_mm", "mx_ok", "ex_ok", "pt_mm"))
        pt_even, pt_odd, av_mm, rinv_ok, pn_ok, own_ok, osum_ok, ot_sb = (
            sem(n) for n in ("pt_even", "pt_odd", "av_mm", "rinv_ok", "pn_ok", "own_ok", "osum_ok", "ot_sb"))
        wo_mm, x1_ok, in_mm, xp_ok = (sem(n) for n in ("wo_mm", "x1_ok", "in_mm", "xp_ok"))
        xs_ok, row_mm, row_sb = (sem(n) for n in ("xs_ok", "row_mm", "row_sb"))
        link_ok = sem("link_ok")
        prep, prep_sqrt, prep_sig, prep_exp, prep_ok = (
            sem(n) for n in ("prep", "prep_sqrt", "prep_sig", "prep_exp", "prep_ok"))
        knp_ok, p1_ok, pr_mm, ret_ok, dlt_ok, outer_ok, arg_ok, tanh_ok, st_ok = (
            sem(n) for n in ("knp_ok", "p1_ok", "pr_mm", "ret_ok", "dlt_ok", "outer_ok", "arg_ok", "tanh_ok", "st_ok"))
        step_in = sem("step_in")
        keep_ok, bs_ok, qp_ok, sq_mm, sq_sb = (sem(n) for n in ("keep_ok", "bs_ok", "qp_ok", "sq_mm", "sq_sb"))
        fin_sig, fin, bo_ok, bt_mm, bt_sb, y_mm, x2_ok = (
            sem(n) for n in ("fin_sig", "fin", "bo_ok", "bt_mm", "bt_sb", "y_mm", "x2_ok"))
        r_mm, rt, rt_exp, gate_ok, gt_mm, gt_sb, b2_mm, acc_init = (
            sem(n) for n in ("r_mm", "rt", "rt_exp", "gate_ok", "gt_mm", "gt_sb", "b2_mm", "acc_init"))
        w_in = [sem(f"w_in{i}") for i in range(2)]
        b1_ok = sem("b1_ok")
        h_mm, h_sb, o_mm, acc_ok, ft_mm, res_ok, stored = (
            sem(n) for n in ("h_mm", "h_sb", "o_mm", "acc_ok", "ft_mm", "res_ok", "stored"))

        def per_group(eng, step, n=NB):
            for b in range(4):
                step(b, b, 0)
            with eng.Fori(1, n // 4 - 1) as i:
                for u in range(4):
                    step(4 * i + u, 4 + u, i)
            for b in range(n - 4, n):
                step(b, b, n // 4 - 1)

        def cols(c, w=CH):
            return slice(c * w, (c + 1) * w)

        block = ctx.enter_context(nc.Block())

        @block.sync
        def _(sp):
            sp.dma_start(cst[:, :], cst_d).then_inc(cst_in, 16)
            sp.dma_start(x[:, :], xT).then_inc(x_in, 16)

            def load_ctx(b, pos, i):
                if pos >= 4:
                    sp.wait_ge(v_mm, b - 3)
                sp.dma_start(ctxr[:, pos % 4, :], ctxT[:, bass.ds(b * S_PAD, S_PAD)]).then_inc(ctx_in[pos % 4], 16)

            per_group(sp, load_ctx)
            def load_expert(e, pos):
                if pos == 0:
                    sp.wait_ge(fin, 4)
                if pos >= 2:
                    sp.wait_ge(o_mm, NC * (e - 1))
                u = pos % 2
                sp.dma_start(w1s[:, u, :], w1_d[:, bass.ds(e * F, F)]).then_inc(w_in[u], 16)
                sp.dma_start(w2s[:, u, :, :], w2_d[:, bass.ds(e * FC, FC), :]).then_inc(w_in[u], 16)

            for e in range(2):
                load_expert(e, e)
            with sp.Fori(1, E // 2) as i:
                for u in range(2):
                    load_expert(2 * i + u, 2 + u)
            for c in range(NC):
                sp.wait_ge(res_ok, c + 1)
                sp.dma_start(out_d[:, cols(c)], res[:, cols(c)]).then_inc(stored, 16)
            sp.wait_ge(stored, 16 * NC)

        @block.tensor
        def _(pe):
            mm, tr = nc.tensor.matmul, nc.tensor.transpose

            def layernorm(s, ready):
                def mean(c):
                    n = NC * s + c
                    pe.wait_ge(ready, ready_at(s, c))
                    if c >= 2:
                        pe.wait_ge(ln_cent, n - 1)
                    mm(bank[c % 2][:, :], C("mean"), x[:, cols(c)], start=True, stop=True).then_inc(ln_mean, 1)

                mean(0)
                for c in range(NC):
                    n = NC * s + c
                    if c + 1 < NC:
                        mean(c + 1)
                    pe.wait_ge(ln_sq, n + 1)
                    if c >= 2:
                        pe.wait_ge(ln_std, n - 1)
                    mm(bank[2 + c % 2][:, :], C("mean"), sq[:, c % 2, :], start=True, stop=True).then_inc(ln_var, 1)

            def ready_at(s, c):
                return 16 if s == 0 else c + 1

            pe.wait_ge(cst_in, 16)
            layernorm(0, x_in)
            for c in range(NC):
                pe.wait_ge(ln_out, c + 1)
                if c >= 2:
                    pe.wait_ge(q_sb, c - 1)
                mm(bank[4 + c % 2][:, :], C("wq"), xn[:, cols(c)], start=True, stop=True).then_inc(q_mm, 1)

            def K(b, pos, fours):
                pe.wait_ge(ctx_in[pos % 4], 16 * fours)
                if pos >= 1:
                    pe.wait_ge(v_sb, b)
                mm(bank[2][:, 0:S_CTX], C("wk"), ctxr[:, pos % 4, 0:S_CTX], start=True, stop=True).then_inc(k_mm, 1)

            def V(b, pos):
                pe.wait_ge(k_sb, b + 1)
                for c in range(NCH):
                    last = mm(bank[2][0:KCH, c * D:(c + 1) * D], ctxr[:, pos % 4, c * KCH:(c + 1) * KCH], C("wv"),
                              start=True, stop=True)
                last.then_inc(v_mm, 1)

            def scores(b, pos, half):
                if half == 0:
                    pe.wait_ge(k_sb, b + 1)
                    pe.wait_ge(qbd_ok, b + 1)
                if pos >= 1:
                    pe.wait_ge(ex_ok, 2 * b + half - 1)
                for g in (2 * half, 2 * half + 1):
                    r = slice(32 * g, 32 * g + 32)
                    last = mm(bank[4 + g][:, 0:S_CTX], qbd[r, pos % 2, :, :], Ksb[r, pos % 2, :], start=True, stop=True)
                last.then_inc(sc_mm, 1)

            def transposes(b, pos, g):
                pe.wait_ge(pn_ok, 2 * b + g // 2 + 1)
                if pos >= 1 or g >= 2:
                    pe.wait_ge(pt_odd if g % 2 else pt_even, 2 * b + g // 2)
                for c in range(NCH):
                    last = tr(bank[g % 2][0:KCH, c * 128:(c + 1) * 128], P[:, pos % 2, g, c * KCH:(c + 1) * KCH],
                              C("ident"))
                last.then_inc(pt_mm, 1)

            def av(b, pos, g, i):
                if g == 0:
                    pe.wait_ge(v_sb, b + 1)
                    if pos >= 4 and pos % 4 == 0:
                        pe.wait_ge(own_ok, i)
                pe.wait_ge(pt_odd if g % 2 else pt_even, 2 * b + g // 2 + 1)
                for c in range(NCH):
                    last = mm(bank[3][32 * g:32 * g + 32, pos % 4 * 128:pos % 4 * 128 + 128],
                              Vsb[:, pos % 4, c, 32 * g:32 * g + 32], PT[:, g, c, :], start=(c == 0), stop=(c == NCH - 1))
                if g == NG - 1:
                    last.then_inc(av_mm, 1)

            def row(b, pos, i):
                if pos < NB - 1:
                    scores(b + 1, pos + 1, 0)
                if pos >= 1:
                    av(b - 1, pos - 1, 2, i)
                    av(b - 1, pos - 1, 3, i)
                if pos < NB - 2:
                    K(b + 2, pos + 2, i + 1 + (pos % 4 >= 2))
                transposes(b, pos, 0)
                transposes(b, pos, 1)
                if pos < NB - 1:
                    scores(b + 1, pos + 1, 1)
                av(b, pos, 0, i)
                av(b, pos, 1, i)
                if pos < NB - 2:
                    V(b + 2, pos + 2)
                transposes(b, pos, 2)
                transposes(b, pos, 3)

            pe.wait_ge(q_sb, NC)
            pe.wait_ge(pads, 2)
            for b in range(2):
                K(b, b, 1)
                V(b, b)
            for half in range(2):
                scores(0, 0, half)
            per_group(pe, row)
            av(NB - 1, NB - 1, 2, 0)
            av(NB - 1, NB - 1, 3, 0)
            for c in range(NC):
                pe.wait_ge(ot_sb, NB // 4)
                if c >= 2:
                    pe.wait_ge(x1_ok, c - 1)
                mm(bank[c % 2][:, :], C("wo"), qT[:, cols(c)], start=True, stop=True).then_inc(wo_mm, 1)

            pe.wait_ge(x1_ok, NC)
            layernorm(1, x1_ok)
            for c in range(NC):
                pe.wait_ge(ln_out, NC + c + 1)
                if c >= 2:
                    pe.wait_ge(xp_ok, c - 1)
                mm(bank[4 + c % 2][:, :], C("win"), xn[:, cols(c)], start=True, stop=True).then_inc(in_mm, 1)

            def row_features(t, pos):
                pe.wait_ge(xs_ok, t + 1)
                if pos >= 2:
                    pe.wait_ge(row_sb, t - 1)
                for n2 in range(2):
                    last = mm(bank[pos % 2][64 * n2:64 * n2 + 64, 0:ROWF], xs[:, pos % 2, :], C(f"wrow{n2}"),
                              start=True, stop=True)
                last.then_inc(row_mm, 1)

            for t in range(2):
                row_features(t, t)
            with pe.Fori(1, T // 2) as i:
                for u in range(2):
                    row_features(2 * i + u, 2 + u)

            def retrieve(t, g):
                pe.wait_ge(p1_ok, 2 * t + g + 1)
                for m in range(0, N_ST, 4):
                    last = mm(bank[1 + g][:, 0:4 * N_ST], C("ident"), P1[:, g, :, m:m + 4],
                              start=(m == 0), stop=(m == N_ST - 4))
                last.then_inc(pr_mm, 1)

            def readout(t, pos, half):
                if half == 0:
                    pe.wait_ge(qp_ok, 2 * t + 2)
                    if pos >= 1:
                        pe.wait_ge(sq_sb, t)
                for m in range(16 * half, 16 * half + 16, 2):
                    last = mm(bank[3][:, 0:4 * N_ST], C("ident"),
                              QP[:, pos % 2, :, :, m:m + 2].rearrange("p g i j -> p (g i) j"),
                              start=(m == 0), stop=(m == N_ST - 2))
                if half:
                    last.then_inc(sq_mm, 1)

            def step(t, pos):
                for g in range(G2):
                    retrieve(t, g)
                if pos >= 2:
                    for half in range(2):
                        readout(t - 2, pos - 2, half)

            for t in range(4):
                step(t, t)
            with pe.Fori(2, T // 2) as i:
                for u in range(2):
                    step(2 * i + u, 4 + u)
            for t in range(T - 2, T):
                for half in range(2):
                    readout(t, t, half)

            pe.wait_ge(bo_ok, 1)
            tb = CH // NB
            for c in range(NC):
                if c >= 2:
                    pe.wait_ge(bt_sb, c - 1)
                for k in range(tb):
                    last = mm(bank[c % 2][0:G2 * N_ST, k * NB:(k + 1) * NB], KN[:, c * tb + k, :, :], C("sum_halves"),
                              start=True, stop=True)
                last.then_inc(bt_mm, 1)
                pe.wait_ge(bt_sb, c + 1)
                if c >= 2:
                    pe.wait_ge(x2_ok, c - 1)
                mm(bank[4 + c % 2][:, :], cst[0:G2 * N_ST, COL["wout"][0]:COL["wout"][1]], boT[:, c % 2, :],
                   start=True, stop=True).then_inc(y_mm, 1)

            pe.wait_ge(x2_ok, NC)
            layernorm(2, x2_ok)
            for k in range(TT):
                pe.wait_ge(ln_out, 2 * NC + k // 4 + 1)
                last = mm(bank[4][:, k * E:(k + 1) * E], xn[:, cols(k, D)], C("wr"), start=True, stop=True)
            last.then_inc(r_mm, 1)
            pe.wait_ge(gate_ok, 1)
            for c in range(NC):
                if c >= 2:
                    pe.wait_ge(gt_sb, c - 1)
                for k in range(4):
                    last = tr(bank[c % 2][0:E, k * 128:(k + 1) * 128], gate[:, 4 * c + k, :], C("ident"))
                last.then_inc(gt_mm, 1)
                pe.wait_ge(gt_sb, c + 1)
                if c >= 2:
                    pe.wait_ge(acc_init, c - 1)
                for k in range(4):
                    last = mm(bank[2 + c % 2][:, k * D:(k + 1) * D], gateT[:, 4 * c + k, :],
                              cst[0:E, COL["b2"][0]:COL["b2"][1]], start=True, stop=True)
                last.then_inc(b2_mm, 1)
            pe.wait_ge(acc_init, NC)

            def expert(e, pos):
                u = pos % 2
                pe.wait_ge(w_in[u], 16 * (e + 2 - u))
                for c in range(NC):
                    n = NC * e + c
                    for f in range(FC):
                        if pos > 0 or c > 0:
                            pe.wait_ge(h_sb, FC * n + f - 3)
                        mm(bank[f][:, :], w1s[:, u, f * D:(f + 1) * D], xn[:, cols(c)],
                           start=True, stop=True).then_inc(h_mm, 1)
                    pe.wait_ge(h_sb, FC * (n + 1))
                    if pos > 0 or c >= 2:
                        pe.wait_ge(acc_ok, n - 1)
                    for k in range(4):
                        for f in range(FC):
                            last = mm(bank[4 + c % 2][:, k * D:(k + 1) * D], hid[:, c % 2, f, k * 128:(k + 1) * 128],
                                      w2s[:, u, f, :], start=(f == 0), stop=(f == FC - 1))
                    last.then_inc(o_mm, 1)

            for e in range(2):
                expert(e, e)
            with pe.Fori(1, E // 2) as i:
                for u in range(2):
                    expert(2 * i + u, 2 + u)
            pe.wait_ge(acc_ok, E * NC)
            for c in range(NC):
                if c >= 2:
                    pe.wait_ge(res_ok, c - 1)
                for k in range(4):
                    last = tr(bank[6 + c % 2][:, k * 128:(k + 1) * 128], acc[:, 4 * c + k, :], C("ident"))
                last.then_inc(ft_mm, 1)

        @block.scalar
        def _(act):
            af = nc.scalar.activation

            def layernorm(s):
                for c in range(NC):
                    n = NC * s + c
                    act.wait_ge(ln_cent, n + 1)
                    if c >= 2:
                        act.wait_ge(ln_var, n - 1)
                    af(sq[:, c % 2, :], xc[:, cols(c)], ACT.Square).then_inc(ln_sq, 1)
                    act.wait_ge(ln_var, n + 1)
                    if c >= 2:
                        act.wait_ge(ln_rstd, n - 1)
                    af(std[:, c % 2, :], bank[2 + c % 2][:, :], ACT.Sqrt, bias=C("eps")).then_inc(ln_std, 1)

            act.wait_ge(cst_in, 16)
            layernorm(0)

            def k_out(b, pos):
                act.wait_ge(k_mm, b + 1)
                if pos >= 2:
                    act.wait_ge(sc_mm, 2 * b - 2)
                af(Ksb[:, pos % 2, :], bank[2][:, 0:S_CTX], ACT.Identity, bias=C("bk")).then_inc(k_sb, 1)

            def v_out(b, pos):
                act.wait_ge(v_mm, b + 1)
                nc.scalar.copy(Vsb[:, pos % 4, :, :].rearrange("k c d -> k (c d)"), bank[2][0:KCH, 0:NCH * D]).then_inc(v_sb, 1)

            def exps(b, pos, half):
                act.wait_ge(mx_ok, 2 * b + half + 1)
                if pos >= 2 and half == 0:
                    act.wait_ge(pt_mm, 4 * b - 4)
                for g in (2 * half, 2 * half + 1):
                    last = af(P[:, pos % 2, g, 0:S_CTX], bank[4 + g][:, 0:S_CTX], ACT.Exp,
                              bias=nmx[:, pos % 2, g:g + 1], accum_out=rsum[:, pos % 2, g:g + 1])
                last.then_inc(ex_ok, 1)

            def pt_out(b, g):
                act.wait_ge(pt_mm, 4 * b + g + 1)
                nc.scalar.copy(PT[:, g, :, :].rearrange("k c q -> k (c q)"), bank[1][0:KCH, 0:NCH * 128]).then_inc(pt_odd, 1)

            def row(b, pos, i):
                if pos < NB - 1:
                    exps(b + 1, pos + 1, 0)
                if pos < NB - 2:
                    k_out(b + 2, pos + 2)
                pt_out(b, 1)
                if pos < NB - 1:
                    exps(b + 1, pos + 1, 1)
                if pos < NB - 2:
                    v_out(b + 2, pos + 2)
                pt_out(b, 3)

            act.wait_ge(pads, 2)
            act.wait_ge(q_sb, NC)
            for b in range(2):
                k_out(b, b)
                v_out(b, b)
            for half in range(2):
                exps(0, 0, half)
            per_group(act, row)

            layernorm(1)
            for c in range(NC):
                act.wait_ge(in_mm, c + 1)
                af(qT[:, cols(c)], bank[4 + c % 2][:, :], ACT.Silu).then_inc(xp_ok, 1)

            def step_tokens(t, pos):
                if pos >= 2:
                    act.wait_ge(row_mm, t - 1)
                nc.scalar.copy(xs[:, pos % 2, :], qT[:, bass.ds(t * NB, NB)]).then_inc(xs_ok, 1)

            act.wait_ge(xp_ok, NC)
            for t in range(2):
                step_tokens(t, t)
            with act.Fori(1, T // 2) as i:
                for u in range(2):
                    step_tokens(2 * i + u, 2 + u)

            act.wait_ge(prep, 3)
            af(nrm2[:, :], nrm[:, :], ACT.Sqrt).then_inc(prep_sqrt, 1)
            af(lexp[:, :, :], lsh[:, :, :], ACT.Exp).then_inc(prep_exp, 1)
            af(BT[:, :, :, :], BT[:, :, :, :], ACT.Sigmoid).then_inc(prep_sig, 1)

            def sq_out(t, pos):
                act.wait_ge(sq_mm, t + 1)
                nc.scalar.copy(SQ2[:, :, bass.ds(t, 1), :].rearrange("p k o x -> p (o x) k"),
                               bank[3][:, 0:4 * N_ST].rearrange("p (x k) -> p x k", k=2)).then_inc(sq_sb, 1)

            def beta_query(t, pos):
                if pos >= 2:
                    act.wait_ge(qp_ok, 2 * t - 2)
                nc.scalar.copy(now[:, pos % 2, 0:2, :], BT[:, bass.ds(t, 1), :, :].rearrange("p o g i -> p (o g) i")).then_inc(step_in, 1)
                nc.scalar.copy(now[:, pos % 2, 2:3, :], rowf[:, bass.ds(t, 1), 192:224]).then_inc(step_in, 1)
                nc.scalar.copy(now[:, pos % 2, 3:5, :],
                               rowf[:, bass.ds(t, 1), 64:128].rearrange("p o (g i) -> p (o g) i", g=2)).then_inc(step_in, 1)

            def step(t, pos):
                for g in range(G2):
                    act.wait_ge(st_ok, 2 * t + g + 1)
                    af(SP[:, g, :, :], S[:, pos % 2, g, :, :], ACT.Copy,
                       scale=omw[:, bass.ds(t, 1), g]).then_inc(keep_ok, 1)
                for g in range(G2):
                    act.wait_ge(arg_ok, 2 * t + g + 1)
                    ps = pair[g][:, :, :].rearrange("p a f -> p (a f)")
                    af(ps, ps, ACT.Tanh).then_inc(tanh_ok, 1)
                if pos < T - 1:
                    beta_query(t + 1, pos + 1)
                if pos >= 2:
                    sq_out(t - 2, pos - 2)

            act.wait_ge(prep_ok, 1)
            act.wait_ge(prep_sig, 1)
            beta_query(0, 0)
            for t in range(2):
                step(t, t)
            with act.Fori(1, T // 2 - 1) as i:
                for u in range(2):
                    step(2 * i + u, 2 + u)
            for t in range(T - 2, T):
                step(t, t)
            for t in range(T - 2, T):
                sq_out(t, t)
            act.wait_ge(fin, 1)
            af(BT[:, :, :, :], SQ[:, :, :, :], ACT.Sigmoid).then_inc(fin_sig, 1)
            for c in range(NC):
                act.wait_ge(bt_mm, c + 1)
                if c >= 2:
                    act.wait_ge(y_mm, c - 1)
                nc.scalar.copy(boT[:, c % 2, :], bank[c % 2][0:G2 * N_ST, :]).then_inc(bt_sb, 1)

            layernorm(2)
            act.wait_ge(rt, 2)
            af(eexp[:, :, :], elog[:, :, :], ACT.Exp).then_inc(rt_exp, 1)

            def expert(e, pos):
                nc.scalar.copy(b1s[:, pos % 2, :], cst[:, bass.ds(e * FC + COL["b1"][0], FC)]).then_inc(b1_ok, 1)
                act.wait_ge(b1_ok, e + 1)
                for c in range(NC):
                    n = NC * e + c
                    if pos > 0 or c >= 2:
                        act.wait_ge(o_mm, n - 1)
                    for f in range(FC):
                        act.wait_ge(h_mm, FC * n + f + 1)
                        af(hid[:, c % 2, f, :], bank[f][:, :], ACT.Gelu,
                           bias=b1s[:, pos % 2, f:f + 1]).then_inc(h_sb, 1)

            for e in range(2):
                expert(e, e)
            with act.Fori(1, E // 2) as i:
                for u in range(2):
                    expert(2 * i + u, 2 + u)

        @block.gpsimd
        def _(pool):
            pool.memset(P[:, :, :, S_CTX:S_PAD], 0.0).then_inc(pads, 1)
            pool.memset(S[:, 0, :, :, :], 0.0).then_inc(pads, 1)
            pool.wait_ge(cst_in, 16)
            pool.wait_ge(q_sb, NC)
            q_tb = qT[:, :].rearrange("p (t b) -> p b t", b=NB)

            def blockdiag(b, pos, i):
                if pos >= 2:
                    pool.wait_ge(sc_mm, 2 * b - 2)
                pool.tensor_tensor(qbd[:, pos % 2, :, :],
                                   q_tb[:, bass.ds(b, 1), :].to_broadcast([D, HG, T]),
                                   C("head_of_row").unsqueeze(2).to_broadcast([D, HG, T]), ALU.mult).then_inc(qbd_ok, 1)

            per_group(pool, blockdiag)
            pool.wait_ge(prep_ok, 1)

            def beta_state(t, pos):
                pool.wait_ge(step_in, 3 * t + 3)
                for g in range(G2):
                    pool.wait_ge(st_ok, 2 * t + g + 1)
                    if pos >= 1:
                        pool.wait_ge(arg_ok, 2 * t + g - 1)
                    pool.tensor_tensor(A[:, g, :, :], S[:, pos % 2, g, :, :],
                                       now[:, pos % 2, g, :].unsqueeze(2).to_broadcast([128, N_ST, N_ST]),
                                       ALU.mult).then_inc(bs_ok, 1)

            def query_state(t, pos):
                for g in range(G2):
                    pool.wait_ge(st_ok, 2 * t + g + 3)
                    if pos >= 2 and g == 0:
                        pool.wait_ge(sq_mm, t - 1)
                    pool.tensor_tensor(QP[:, pos % 2, g, :, :], S[:, (pos + 1) % 2, g, :, :],
                                       now[:, pos % 2, 2:3, :].to_broadcast([128, N_ST, N_ST]),
                                       ALU.mult).then_inc(qp_ok, 1)

            def step(t, pos):
                if pos < T - 1:
                    beta_state(t + 1, pos + 1)
                query_state(t, pos)

            beta_state(0, 0)
            for t in range(2):
                step(t, t)
            with pool.Fori(1, T // 2 - 1) as i:
                for u in range(2):
                    step(2 * i + u, 2 + u)
            for t in range(T - 2, T):
                step(t, t)

        @block.vector
        def _(dve):
            v = nc.vector

            def layernorm(s):
                def centre(c):
                    dve.wait_ge(ln_mean, NC * s + c + 1)
                    v.tensor_tensor(xc[:, cols(c)], x[:, cols(c)], bank[c % 2][:, :], ALU.subtract).then_inc(ln_cent, 1)

                centre(0)
                for c in range(NC):
                    n = NC * s + c
                    if c + 1 < NC:
                        centre(c + 1)
                    dve.wait_ge(ln_std, n + 1)
                    v.reciprocal(std[:, c % 2, :], std[:, c % 2, :]).then_inc(ln_rstd, 1)
                    dve.wait_ge(ln_rstd, n + 1)
                    v.tensor_tensor(xn[:, cols(c)], xc[:, cols(c)], std[:, c % 2, :], ALU.mult).then_inc(ln_out, 1)

            dve.wait_ge(cst_in, 16)
            dve.wait_ge(x_in, 16)
            layernorm(0)
            for c in range(NC):
                dve.wait_ge(q_mm, c + 1)
                v.tensor_scalar(qT[:, cols(c)], bank[4 + c % 2][:, :], C("bq"), DH ** -0.5, ALU.add, ALU.mult).then_inc(q_sb, 1)

            def maxes(b, pos, half):
                dve.wait_ge(sc_mm, 2 * b + half + 1)
                v.tensor_reduce(nmx[:, pos % 2, 2 * half:2 * half + 2], pair[half][:, :, 0:S_CTX], AX.X, ALU.max,
                                negate=True).then_inc(mx_ok, 1)

            def pt_out(b, g):
                dve.wait_ge(pt_mm, 4 * b + g + 1)
                v.tensor_copy(PT[:, g, :, :].rearrange("k c q -> k (c q)"), bank[0][0:KCH, 0:NCH * 128]).then_inc(pt_even, 1)

            def inverse_sums(b, pos, half):
                h = slice(2 * half, 2 * half + 2)
                dve.wait_ge(ex_ok, 2 * b + half + 1)
                v.reciprocal(rinv[:, h], rsum[:, pos % 2, h]).then_inc(rinv_ok, 1)

            def normalise(b, pos, half):
                dve.wait_ge(rinv_ok, 2 * b + half + 1)
                for g in (2 * half, 2 * half + 1):
                    last = v.tensor_scalar(P[:, pos % 2, g, 0:S_CTX], P[:, pos % 2, g, 0:S_CTX], rinv[:, g:g + 1], None,
                                           ALU.mult)
                last.then_inc(pn_ok, 1)

            o_tb = qT[:, :].rearrange("p (t b) -> p b t", b=NB)

            def own_heads(b):
                dve.wait_ge(av_mm, b + 1)
                v.tensor_tensor(avm[:, :].rearrange("p (r h q) -> p r h q", r=4, h=HG),
                                bank[3][:, :].rearrange("p (r h q) -> p r h q", r=4, h=HG),
                                C("head_of_row").unsqueeze(1).unsqueeze(3).to_broadcast([D, 4, HG, T]),
                                ALU.mult).then_inc(own_ok, 1)

            def sum_heads(n):
                dve.wait_ge(own_ok, n)
                v.tensor_reduce(osum[:, :, :], avm[:, :].rearrange("p (r h q) -> p r q h", r=4, h=HG), AX.X,
                                ALU.add).then_inc(osum_ok, 1)

            def heads_out(b, n):
                dve.wait_ge(osum_ok, n)
                v.tensor_scalar(o_tb[:, bass.ds(b - 3, 4), :], osum[:, :, :], C("bv"), None, ALU.add).then_inc(ot_sb, 1)

            def row(b, pos, i):
                if pos < NB - 1:
                    maxes(b + 1, pos + 1, 0)
                four_done = pos % 4 == 0 and pos > 0
                if four_done:
                    own_heads(b - 1)
                pt_out(b, 0)
                if four_done:
                    sum_heads(i)
                if pos < NB - 1:
                    maxes(b + 1, pos + 1, 1)
                    inverse_sums(b + 1, pos + 1, 0)
                if four_done:
                    heads_out(b - 1, i)
                if pos < NB - 1:
                    normalise(b + 1, pos + 1, 0)
                    inverse_sums(b + 1, pos + 1, 1)
                pt_out(b, 2)
                if pos < NB - 1:
                    normalise(b + 1, pos + 1, 1)

            for half in range(2):
                maxes(0, 0, half)
            for half in range(2):
                inverse_sums(0, 0, half)
                normalise(0, 0, half)
            per_group(dve, row)
            own_heads(NB - 1)
            sum_heads(NB // 4)
            heads_out(NB - 1, NB // 4)
            for c in range(NC):
                dve.wait_ge(wo_mm, c + 1)
                v.scalar_tensor_tensor(x[:, cols(c)], bank[c % 2][:, :], C("bo"), x[:, cols(c)], ALU.add,
                                       ALU.add).then_inc(x1_ok, 1)

            layernorm(1)

            def row_out(t, pos):
                dve.wait_ge(row_mm, t + 1)
                v.tensor_copy(rowf[:, bass.ds(t, 1), :].rearrange("p o f -> p (o f)"), bank[pos % 2][:, 0:ROWF]).then_inc(row_sb, 1)

            for t in range(2):
                row_out(t, t)
            with dve.Fori(1, T // 2) as i:
                for u in range(2):
                    row_out(2 * i + u, 2 + u)

            chain = [0]

            def link(ins):
                chain[0] += 1
                ins.then_inc(link_ok, 1)
                dve.wait_ge(link_ok, chain[0])

            dve.wait_ge(row_sb, T)
            kraw = rowf[:, :, 0:64].rearrange("p t (g j) -> p t g j", g=G2)
            logit = rowf[:, :, 224:228]
            link(v.tensor_tensor(KN[:, :, :, :], kraw, kraw, ALU.mult))
            v.tensor_reduce(nrm[:, :], KN[:, :, :, :].rearrange("p t g j -> p (t g) j"), AX.X, ALU.add).then_inc(prep, 1)
            v.tensor_tensor(BT[:, :, :, :].rearrange("p t g i -> p t (g i)"), rowf[:, :, 128:192],
                            C("bbeta").unsqueeze(1).to_broadcast([128, T, G2 * N_ST]), ALU.add).then_inc(prep, 1)
            link(v.tensor_reduce(lmax[:, :], logit, AX.X, ALU.max))
            v.tensor_tensor(lsh[:, :, :], logit, lmax[:, :].unsqueeze(2).to_broadcast([128, T, BLK]),
                            ALU.subtract).then_inc(prep, 1)
            lm = logit.unsqueeze(2).to_broadcast([128, T, BLK, BLK])
            ln = logit.unsqueeze(3).to_broadcast([128, T, BLK, BLK])

            def tri(name):
                return C(name).rearrange("p (n m) -> p n m", m=BLK).unsqueeze(1).to_broadcast([128, T, BLK, BLK])

            v.tensor_tensor(cmpa[:, :, :, :], lm, ln, ALU.is_ge).then_inc(link_ok, 1)
            v.tensor_tensor(cmpb[:, :, :, :], lm, ln, ALU.is_gt).then_inc(link_ok, 1)
            chain[0] += 2
            dve.wait_ge(link_ok, chain[0])
            v.tensor_tensor(cmpa[:, :, :, :], cmpa[:, :, :, :], tri("low4"), ALU.mult).then_inc(link_ok, 1)
            v.tensor_tensor(cmpb[:, :, :, :], cmpb[:, :, :, :], tri("up4"), ALU.mult).then_inc(link_ok, 1)
            chain[0] += 2
            dve.wait_ge(link_ok, chain[0])
            link(v.tensor_tensor(cmpa[:, :, :, :], cmpa[:, :, :, :], cmpb[:, :, :, :], ALU.add))
            link(v.tensor_reduce(rank[:, :, :], cmpa[:, :, :, :], AX.X, ALU.add))
            link(v.tensor_scalar(msel[:, :, :], rank[:, :, :], 2.0, None, ALU.is_lt))
            dve.wait_ge(prep_exp, 1)
            link(v.tensor_reduce(lsum[:, :], lexp[:, :, :], AX.X, ALU.add))
            link(v.reciprocal(linv[:, :], lsum[:, :]))
            link(v.tensor_tensor(sm[:, :, :], lexp[:, :, :], linv[:, :].unsqueeze(2).to_broadcast([128, T, BLK]), ALU.mult))
            link(v.tensor_tensor(msel[:, :, :], msel[:, :, :], sm[:, :, :], ALU.mult))
            link(v.tensor_reduce(usum[:, :], msel[:, :, :], AX.X, ALU.add))
            link(v.tensor_scalar(usum[:, :], usum[:, :], 1e-8, None, ALU.add))
            link(v.reciprocal(uinv[:, :], usum[:, :]))
            link(v.tensor_tensor(uw[:, :, :], msel[:, :, :], uinv[:, :].unsqueeze(2).to_broadcast([128, T, BLK]), ALU.mult))
            for n2 in range(2):
                half = slice(64 * n2, 64 * n2 + 64)
                link(v.tensor_copy(wown[half, :, :], uw[half, :, n2::2]))
                link(v.tensor_copy(smo[half, :, :], sm[half, :, n2::2]))
            link(v.tensor_scalar(omw[:, :, :], wown[:, :, :], -1.0, 1.0, ALU.mult, ALU.add))
            dve.wait_ge(prep_sqrt, 1)
            link(v.tensor_scalar(nrm3[:, :], nrm2[:, :], 1e-6, None, ALU.add))
            link(v.reciprocal(nrm3[:, :], nrm3[:, :]))
            link(v.tensor_tensor(KN[:, :, :, :], kraw,
                                 nrm3[:, :].rearrange("p (t g) -> p t g", g=G2).unsqueeze(3).to_broadcast([128, T, G2, N_ST]),
                                 ALU.mult))
            dve.wait_ge(prep_sig, 1)
            dve.wait_ge(pads, 2)
            v.tensor_copy(nrm2[:, 0:1], nrm3[:, 0:1]).then_inc(prep_ok, 1)
            for g in range(G2):
                v.tensor_copy(nrm[:, g:g + 1], nrm3[:, g:g + 1]).then_inc(st_ok, 1)

            def flat(ap):
                return ap.rearrange("p i j -> p (i j)")

            def keys(t, pos):
                v.tensor_copy(bank[0][:, pos % 2 * 64:pos % 2 * 64 + 64],
                              KN[:, bass.ds(t, 1), :, :].rearrange("p o g j -> p (o g j)")).then_inc(knp_ok, 1)

            def key_rows(pos, g):
                c = pos % 2 * 64 + g * N_ST
                return bank[0][:, c:c + N_ST].unsqueeze(1).to_broadcast([128, N_ST, N_ST])

            def state_keys(t, pos, g):
                dve.wait_ge(knp_ok, t + 1)
                dve.wait_ge(st_ok, 2 * t + g + 1)
                v.tensor_tensor(P1[:, g, :, :], S[:, pos % 2, g, :, :], key_rows(pos, g), ALU.mult).then_inc(p1_ok, 1)

            def blend(t, pos, g):
                n = 2 * t + g + 1
                dve.wait_ge(tanh_ok, n)
                dve.wait_ge(keep_ok, n)
                if pos >= 2:
                    dve.wait_ge(qp_ok, n - 4)
                v.scalar_tensor_tensor(flat(S[:, (pos + 1) % 2, g, :, :]), pair[g][:, :, :].rearrange("p a f -> p (a f)"),
                                       wown[:, bass.ds(t, 1), g], flat(SP[:, g, :, :]), ALU.mult, ALU.add).then_inc(st_ok, 1)

            def subtract_sum(t, pos, g):
                n = 2 * t + g + 1
                if g == 0:
                    dve.wait_ge(step_in, 3 * t + 3)
                dve.wait_ge(pr_mm, n)
                v.tensor_reduce(ret[:, g, :], bank[1 + g][:, 0:4 * N_ST].rearrange("p (i m) -> p i m", m=4), AX.X,
                                ALU.add).then_inc(ret_ok, 1)
                dve.wait_ge(ret_ok, n)
                v.tensor_tensor(dlt[:, g, :], now[:, pos % 2, 3 + g, :], ret[:, g, :], ALU.subtract).then_inc(dlt_ok, 1)

            def outer(t, pos, g):
                dve.wait_ge(dlt_ok, 2 * t + g + 1)
                v.tensor_tensor(pair[g][:, :, :].rearrange("p a (i j) -> p (a i) j", j=N_ST),
                                dlt[:, g, :].unsqueeze(2).to_broadcast([128, N_ST, N_ST]), key_rows(pos, g),
                                ALU.mult).then_inc(outer_ok, 1)

            def argument(t, g):
                n = 2 * t + g + 1
                dve.wait_ge(outer_ok, n)
                dve.wait_ge(bs_ok, n)
                psg = pair[g][:, :, :].rearrange("p a (i j) -> p (a i) j", j=N_ST)
                v.tensor_tensor(psg, psg, A[:, g, :, :], ALU.add).then_inc(arg_ok, 1)

            def step(t, pos):
                state_keys(t, pos, 0)
                if pos >= 1:
                    blend(t - 1, pos - 1, 1)
                state_keys(t, pos, 1)
                subtract_sum(t, pos, 0)
                outer(t, pos, 0)
                if pos < T - 1:
                    keys(t + 1, pos + 1)
                argument(t, 0)
                subtract_sum(t, pos, 1)
                outer(t, pos, 1)
                blend(t, pos, 0)
                argument(t, 1)

            keys(0, 0)
            for t in range(4):
                step(t, t)
            with dve.Fori(2, T // 2 - 1) as i:
                for u in range(2):
                    step(2 * i + u, 4 + u)
            for t in range(T - 2, T):
                step(t, t)
            blend(T - 1, T - 1, 1)

            dve.wait_ge(sq_sb, T)
            v.tensor_tensor(SQ[:, :, :, :].rearrange("p t g i -> p (t g i)"), SQ2[:, 0, :, :].rearrange("p t x -> p (t x)"),
                            SQ2[:, 1, :, :].rearrange("p t x -> p (t x)"), ALU.add).then_inc(fin, 1)
            dve.wait_ge(fin, 1)
            v.tensor_tensor(KN[:, :, :, :], SQ[:, :, :, :], SQ[:, :, :, :], ALU.mult).then_inc(fin, 1)
            dve.wait_ge(fin, 2)
            dve.wait_ge(fin_sig, 1)
            v.tensor_tensor(KN[:, :, :, :], KN[:, :, :, :], BT[:, :, :, :], ALU.mult).then_inc(fin, 1)
            dve.wait_ge(fin, 3)
            v.tensor_tensor(KN[:, :, :, :], KN[:, :, :, :], smo[:, :, :].unsqueeze(3).to_broadcast([128, T, G2, N_ST]),
                            ALU.mult).then_inc(bo_ok, 1)
            dve.wait_ge(bo_ok, 1)
            v.tensor_copy(nrm[:, 0:1], nrm3[:, 0:1]).then_inc(fin, 1)
            for c in range(NC):
                dve.wait_ge(y_mm, c + 1)
                v.tensor_tensor(x[:, cols(c)], x[:, cols(c)], bank[4 + c % 2][:, :], ALU.add).then_inc(x2_ok, 1)

            layernorm(2)
            dve.wait_ge(r_mm, 1)
            lg = bank[4][:, 0:TT * E].rearrange("p (t e) -> p t e", e=E)
            link(v.tensor_reduce(emax[:, :], lg, AX.X, ALU.max))
            v.tensor_tensor(eeq[:, :, :], lg, emax[:, :].unsqueeze(2).to_broadcast([128, TT, E]), ALU.is_ge).then_inc(rt, 1)
            v.tensor_tensor(elog[:, :, :], lg, emax[:, :].unsqueeze(2).to_broadcast([128, TT, E]), ALU.subtract).then_inc(rt, 1)
            dve.wait_ge(rt, 2)
            link(v.tensor_tensor(ecmp[:, :, :, :], eeq[:, :, :].unsqueeze(2).to_broadcast([128, TT, E, E]),
                                 C("low8").rearrange("p (n m) -> p n m", m=E).unsqueeze(1).to_broadcast([128, TT, E, E]),
                                 ALU.mult))
            link(v.tensor_reduce(ecnt[:, :, :], ecmp[:, :, :, :], AX.X, ALU.add))
            link(v.tensor_scalar(ecnt[:, :, :], ecnt[:, :, :], 1.0, None, ALU.is_lt))
            link(v.tensor_tensor(eeq[:, :, :], eeq[:, :, :], ecnt[:, :, :], ALU.mult))
            dve.wait_ge(rt_exp, 1)
            link(v.tensor_reduce(esum[:, :], eexp[:, :, :], AX.X, ALU.add))
            link(v.reciprocal(pmax[:, :], esum[:, :]))
            v.tensor_tensor(gate[:, :, :], eeq[:, :, :], pmax[:, :].unsqueeze(2).to_broadcast([128, TT, E]),
                            ALU.mult).then_inc(gate_ok, 1)
            dve.wait_ge(gate_ok, 1)
            for c in range(NC):
                dve.wait_ge(gt_mm, c + 1)
                v.tensor_copy(gateT[:, 4 * c:4 * c + 4, :].rearrange("e k q -> e (k q)"), bank[c % 2][0:E, :]).then_inc(gt_sb, 1)
                dve.wait_ge(b2_mm, c + 1)
                v.tensor_copy(acc[:, 4 * c:4 * c + 4, :].rearrange("p k d -> p (k d)"), bank[2 + c % 2][:, :]).then_inc(acc_init, 1)
            dve.wait_ge(acc_init, NC)

            def expert(e, pos):
                for c in range(NC):
                    n = NC * e + c
                    dve.wait_ge(o_mm, n + 1)
                    if pos > 0:
                        dve.wait_ge(acc_ok, n - (NC - 1))
                    for k in range(4):
                        last = v.scalar_tensor_tensor(acc[:, 4 * c + k, :], bank[4 + c % 2][:, k * D:(k + 1) * D],
                                                      gate[:, 4 * c + k, bass.ds(e, 1)], acc[:, 4 * c + k, :],
                                                      ALU.mult, ALU.add)
                    last.then_inc(acc_ok, 1)

            for e in range(2):
                expert(e, e)
            with dve.Fori(1, E // 2) as i:
                for u in range(2):
                    expert(2 * i + u, 2 + u)
            for c in range(NC):
                dve.wait_ge(ft_mm, c + 1)
                v.tensor_tensor(res[:, cols(c)], x[:, cols(c)], bank[6 + c % 2][:, :], ALU.add).then_inc(res_ok, 1)


def kernel(x, ctx_1024, L0_xattn_Wq, L0_xattn_bq, L0_xattn_Wk, L0_xattn_bk, L0_xattn_Wv, L0_xattn_bv, L0_xattn_Wo,
           L0_xattn_bo, L0_attn_W_in, L0_attn_W_router, L0_attn_W_kv, L0_attn_W_beta, L0_attn_b_beta, L0_attn_W_q,
           L0_attn_W_out, L0_ffn_Wr, L0_ffn_W1, L0_ffn_b1, L0_ffn_W2, L0_ffn_b2):
    import concourse.bacc as bacc
    from concourse.bass_utils import run_bass_kernel_spmd

    f = np.float32
    n = np.asarray
    xT = n(x).transpose(2, 1, 0).reshape(D, TOK)
    ctxT = np.zeros((D, NB, S_PAD), f)
    ctxT[:, :, :S_CTX] = n(ctx_1024).transpose(2, 0, 1)
    kv = n(L0_attn_W_kv).reshape(BLK, 2, N_ST, D)
    beta = n(L0_attn_W_beta).reshape(BLK, N_ST, D)
    c = np.zeros((128, NCONST), f)

    def put(name, a):
        c[:a.shape[0], COL[name][0]:COL[name][1]] = a

    put("wq", n(L0_xattn_Wq).T)
    put("wk", n(L0_xattn_Wk).T)
    put("wv", n(L0_xattn_Wv).T)
    put("wo", n(L0_xattn_Wo).T)
    put("win", n(L0_attn_W_in).T)
    for h in range(2):
        rows = [kv[h, 0], kv[h + 2, 0], kv[h, 1], kv[h + 2, 1], beta[h], beta[h + 2], n(L0_attn_W_q), n(L0_attn_W_router)]
        put(f"wrow{h}", np.concatenate(rows, 0).T)
    put("wr", n(L0_ffn_Wr))
    p = np.arange(128)
    put("ident", np.eye(128, dtype=f))
    put("mean", np.full((128, 128), 1.0 / D, f))
    put("head_of_row", (p[:, None] // DH % HG == np.arange(HG)).astype(f))
    put("own_head", (p[:, None] // T == np.arange(HG)).astype(f))
    put("sum_heads", (p[:, None] % T == np.arange(T)).astype(f))
    put("sum_halves", (p[:, None] % NB == np.arange(NB)).astype(f))
    put("bq", n(L0_xattn_bq)[:, None])
    put("bk", n(L0_xattn_bk)[:, None])
    put("bv", n(L0_xattn_bv)[:, None])
    put("bo", n(L0_xattn_bo)[:, None])
    bb = n(L0_attn_b_beta)
    put("bbeta", np.repeat(np.stack([np.concatenate([bb[0], bb[2]]), np.concatenate([bb[1], bb[3]])]), NB, 0))
    put("wout", np.tile(n(L0_attn_W_out).T, (G2, 1)))
    put("low4", np.tile(np.tril(np.ones((4, 4), f), -1).reshape(1, 16), (128, 1)))
    put("up4", np.tile(np.triu(np.ones((4, 4), f), 1).reshape(1, 16), (128, 1)))
    put("low8", np.tile(np.tril(np.ones((8, 8), f), -1).reshape(1, 64), (128, 1)))
    put("b1", n(L0_ffn_b1).reshape(E * FC, D).T)
    put("b2", n(L0_ffn_b2))
    put("eps", np.full((128, 1), 1e-5, f))
    w1 = n(L0_ffn_W1).transpose(1, 0, 2).reshape(D, E * F)
    w2 = n(L0_ffn_W2).reshape(E, FC, D, D).transpose(2, 0, 1, 3).reshape(D, E * FC, D)

    nc = bacc.Bacc("TRN2", target_bir_lowering=False, num_devices=1)
    arrays, args = {}, []
    for name, a in [("xT", xT), ("ctxT", ctxT.reshape(D, NB * S_PAD)), ("cst", c), ("w1", w1), ("w2", w2)]:
        a = np.ascontiguousarray(a)
        arrays[f"in_{name}_dram"] = a
        args.append(nc.dram_tensor(f"in_{name}_dram", a.shape, mybir.dt.from_np(a.dtype), kind="ExternalInput").ap())
    args.append(nc.dram_tensor("out_dram", (D, TOK), mybir.dt.float32, kind="ExternalOutput").ap())
    build(nc, *args)
    r = run_bass_kernel_spmd(nc, [arrays], core_ids=[0])
    return np.ascontiguousarray(r.results[0]["out_dram"].reshape(D, T, NB).transpose(2, 1, 0))
```

```python
from contextlib import ExitStack

import numpy as np

import concourse.bass as bass
from concourse import mybir

NB = 64
T = 32
D = 128
TOK = NB * T
S_CTX = 257
KCH = 86
NCH = 3
S_PAD = KCH * NCH
H = 16
DH = D // H
HG = 4
NG = H // HG
N_ST = 32
BLK = 4
G2 = 2
ST = N_ST * N_ST
ROWF = 2 * N_ST * 3 + N_ST + BLK
E = 8
F = 512
FC = F // D
CH = 512
NC = TOK // CH
TT = TOK // D
SLT = TT + E - 1
ROW = 2 * D + 2

_FIRST = [("mean", D), ("ident", D), ("eps", 1), ("wq", D), ("wk", D), ("wv", D), ("bq", 1), ("bk", 1), ("bv", 1),
          ("head_of_row", HG)]
_REST = [("wo", D), ("bo", 1), ("win", D), ("wrow0", ROWF), ("wrow1", ROWF), ("wr", E), ("minus", D), ("sum_halves", NB),
         ("bbeta", G2 * N_ST), ("wout", D), ("low4", 16), ("up4", 16), ("falling", E), ("b1", E * FC), ("b2all", E * D),
         ("before", D), ("ones", D), ("tok_no", TT), ("zeros", D), ("pad_tail", SLT * 2), ("tile_start", TT),
         ("tile_no", SLT)]
_COLS = _FIRST + _REST
NFIRST = sum(w for _, w in _FIRST)
COL, _at = {}, 0
for _n, _w in _COLS:
    COL[_n] = (_at, _at + _w)
    _at += _w
NCONST = _at


def build(nc, xT, ctxT, cst_d, w1_d, w2_d, out_d, sorted_d):
    fp32, uint32 = mybir.dt.float32, mybir.dt.uint32
    ALU = mybir.AluOpType
    ACT = mybir.ActivationFunctionType
    AX = mybir.AxisListType

    with ExitStack() as ctx:
        def sb(name, shape, dtype=fp32):
            return ctx.enter_context(nc.sbuf_tensor(name, shape, dtype))

        def sem(name):
            return ctx.enter_context(nc.semaphore(name))

        bank = [ctx.enter_context(nc.psum_tensor(f"bank{i}", [128, 512], fp32)) for i in range(4)]
        pair = [ctx.enter_context(nc.psum_tensor(f"pair{i}", [128, 2, 512], fp32)) for i in range(2)]
        bank += [pair[0][:, 0, :], pair[0][:, 1, :], pair[1][:, 0, :], pair[1][:, 1, :]]

        ln_bank = [bank[i] for i in (2, 3, 6, 7)]

        cst = sb("cst", [128, NCONST])

        def C(name):
            return cst[:, COL[name][0]:COL[name][1]]

        x = sb("x", [D, TOK])
        xcn = sb("xcn", [D, 2, TOK])
        xc, xn = xcn[:, 0, :], xcn[:, 1, :]
        std = sb("std", [128, TT])
        rstd = sb("rstd", [128, TT])
        qT = sb("qT", [D, TOK])
        ctxr = sb("ctxr", [D, 4, S_PAD])
        Ksb = sb("Ksb", [D, 2, S_CTX])
        Vsb = sb("Vsb", [KCH, 4, NCH, D])
        qbd = sb("qbd", [D, 2, HG, T])
        P = sb("P", [128, 2, NG, S_PAD])
        PT = sb("PT", [KCH, NG, NCH, 128])
        nmx = sb("nmx", [128, 2, NG])
        rsum = sb("rsum", [128, 2, NG])
        rinv = sb("rinv", [128, NG])
        avm = sb("avm", [128, 512])
        osum = sb("osum", [128, 4, T])
        rowf = sb("rowf", [128, T, ROWF])
        KN = sb("KN", [128, T, G2, N_ST])
        BT = sb("BT", [128, T, G2, N_ST])
        nrm = sb("nrm", [128, T * G2])
        nrm2 = sb("nrm2", [128, T * G2])
        nrm3 = sb("nrm3", [128, T * G2])
        lmax = sb("lmax", [128, T])
        lsh = sb("lsh", [128, T, BLK])
        lexp = sb("lexp", [128, T, BLK])
        lsum = sb("lsum", [128, T])
        linv = sb("linv", [128, T])
        sm = sb("sm", [128, T, BLK])
        cmpa = sb("cmpa", [128, T, BLK, BLK])
        cmpb = sb("cmpb", [128, T, BLK, BLK])
        rank = sb("rank", [128, T, BLK])
        msel = sb("msel", [128, T, BLK])
        usum = sb("usum", [128, T])
        uinv = sb("uinv", [128, T])
        wown = sb("wown", [128, T, G2])
        omw = sb("omw", [128, T, G2])
        smo = sb("smo", [128, T, G2])
        S = sb("S", [128, 2, G2, N_ST, N_ST])
        SP = sb("SP", [128, G2, N_ST, N_ST])
        A = sb("A", [128, G2, N_ST, N_ST])
        P1 = sb("P1", [128, G2, N_ST, N_ST])
        QP = sb("QP", [128, 2, G2, N_ST, N_ST])
        now = sb("now", [128, 2, 3, N_ST])
        dlt = sb("dlt", [128, G2, N_ST])
        SQ = P1[:, :, :, :].rearrange("p g i j -> p (g i j)").rearrange("p (t g i) -> p t g i", t=T, g=G2)
        SQ2 = xcn[:, :, :].rearrange("p k (t x) -> p k t x", t=T)
        boT = sb("boT", [G2 * N_ST, 2, CH])
        w1s = P[:, :, :, :].rearrange("p a b c -> p (a b c)")[:, 0:4 * F].rearrange("p (a f) -> p a f", a=4)
        w2s = KN[:, :, :, :].rearrange("p t g j -> p (t g j)").rearrange("p (a f) -> p a f", a=4)
        w1all = S[:, :, :, :, :].rearrange("p a g i j -> p (a g i j)")
        w2all = xcn[:, :, :].rearrange("p k t -> p (k t)")
        hid = A[:, 0, :, :].rearrange("p i j -> p (i j)").rearrange("p (a f q) -> p a f q", a=2, f=FC)
        tok_row = rowf[:, :, :].rearrange("p a b -> p (a b)")[:, 0:TT * ROW].rearrange("p (k r) -> p k r", k=TT)
        sorted_in = sb("sorted_in", [128, 4, ROW])
        xTs = sb("xTs", [D, 2, D])
        b1s = sb("b1s", [128, 4, FC])
        base = sb("base", [128, 4, D])
        ysb = sb("ysb", [128, 4, D])
        prob = sb("prob", [128, 4])
        dest = sb("dest", [128, SLT], uint32)
        elog = sb("elog", [128, TT, E])
        emax = sb("emax", [128, TT])
        eexp = sb("eexp", [128, TT, E])
        esum = sb("esum", [128, TT])
        eeq = sb("eeq", [128, TT, E])
        efirst = sb("efirst", [128, TT])
        cum = sb("cum", [128, 2, TT, E])
        tot = sb("tot", [128, TT, E])
        epos = sb("epos", [128, TT, E])
        tcmp = sb("tcmp", [128, E, TT])
        tiles = sb("tiles", [128, E])
        tend = sb("tend", [128, 2, E])
        tbase = sb("tbase", [128, E])
        ecmp2 = sb("ecmp2", [128, SLT, E])
        tile_ex = sb("tile_ex", [128, SLT])
        tile_exu = sb("tile_exu", [128, SLT], uint32)
        slot = sb("slot", [128, TT])
        slotu = sb("slotu", [128, TT], uint32)

        cst_in, rest_in = sem("cst_in"), sem("rest_in")
        x_in = [sem(f"x_in{c}") for c in range(NC)]
        ctx_in = [sem(f"ctx_in{i}") for i in range(4)]
        pads = sem("pads")
        ln_mean, ln_cent, ln_sq, ln_var, ln_std, ln_rstd, ln_spread, ln_out = (
            sem(n) for n in ("ln_mean", "ln_cent", "ln_sq", "ln_var", "ln_std", "ln_rstd", "ln_spread", "ln_out"))
        q_mm, q_sb = sem("q_mm"), sem("q_sb")
        k_mm, k_sb, v_mm, v_sb, qbd_ok = (sem(n) for n in ("k_mm", "k_sb", "v_mm", "v_sb", "qbd_ok"))
        sc_mm, mx_ok, ex_ok, pt_mm = (sem(n) for n in ("sc_mm", "mx_ok", "ex_ok", "pt_mm"))
        pt_even, pt_odd, av_mm, rinv_ok, pn_ok, own_ok, osum_ok, ot_sb = (
            sem(n) for n in ("pt_even", "pt_odd", "av_mm", "rinv_ok", "pn_ok", "own_ok", "osum_ok", "ot_sb"))
        wo_mm, x1_ok, in_mm, xp_ok = (sem(n) for n in ("wo_mm", "x1_ok", "in_mm", "xp_ok"))
        row_mm, row_sb = sem("row_mm"), sem("row_sb")
        link_ok = sem("link_ok")
        ksq_ok, bias_ok, cmp_ok, tri_ok, rank_ok = (sem(n) for n in ("ksq_ok", "bias_ok", "cmp_ok", "tri_ok", "rank_ok"))
        prep, prep_sqrt, prep_sig, prep_exp, prep_ok = (
            sem(n) for n in ("prep", "prep_sqrt", "prep_sig", "prep_exp", "prep_ok"))
        knp_ok, p1_ok, pr_mm, dlt_ok, outer_ok, arg_ok, tanh_ok, st_ok = (
            sem(n) for n in ("knp_ok", "p1_ok", "pr_mm", "dlt_ok", "outer_ok", "arg_ok", "tanh_ok", "st_ok"))
        step_in = sem("step_in")
        bs_ok, qp_ok, sq_mm, sq_sb = (sem(n) for n in ("bs_ok", "qp_ok", "sq_mm", "sq_sb"))
        sq_ok, sqr_ok, wsq_ok = sem("sq_ok"), sem("sqr_ok"), sem("wsq_ok")
        fin_sig, bo_ok, bt_mm, bt_sb, y_mm, x2_ok = (
            sem(n) for n in ("fin_sig", "bo_ok", "bt_mm", "bt_sb", "y_mm", "x2_ok"))
        r_mm, rt, rt_exp, best_ok, count_mm, slot_ok, tx_mm, tx_sb, row_ok = (
            sem(n) for n in ("r_mm", "rt", "rt_exp", "best_ok", "count_mm", "slot_ok", "tx_mm", "tx_sb", "row_ok"))
        w1_in, w2_in, pad_out, sorted_out = (sem(n) for n in ("w1_in", "w2_in", "pad_out", "sorted_out"))
        tile_in = [sem(f"tile_in{i}") for i in range(4)]
        stored = [sem(f"stored{i}") for i in range(4)]
        w_ok, base_ok, xt_mm, xt_sb, h_mm, h_sb, e_mm, e_sb = (
            sem(n) for n in ("w_ok", "base_ok", "xt_mm", "xt_sb", "h_mm", "h_sb", "e_mm", "e_sb"))

        def per_group(eng, step, n=NB):
            for b in range(4):
                step(b, b, 0)
            with eng.Fori(1, n // 4 - 1) as i:
                for u in range(4):
                    step(4 * i + u, 4 + u, i)
            for b in range(n - 4, n):
                step(b, b, n // 4 - 1)

        def per_tile(eng, step):
            for j in range(4):
                step(j, j, 0)
            with eng.Fori(1, SLT // 4) as i:
                for u in range(4):
                    step(4 * i + u, 4 + u, i)
            for j in range(SLT // 4 * 4, SLT):
                step(j, j, j // 4)

        def cols(c, w=CH):
            return slice(c * w, (c + 1) * w)

        block = ctx.enter_context(nc.Block())

        @block.sync
        def _(sp):
            sp.dma_start(cst[:, 0:NFIRST], cst_d[:, 0:NFIRST]).then_inc(cst_in, 16)
            for c in range(NC):
                sp.dma_start(x[:, cols(c)], xT[:, cols(c)]).then_inc(x_in[c], 16)

            def load_ctx(b, pos, i):
                if pos >= 4:
                    sp.wait_ge(v_mm, b - 3)
                sp.dma_start(ctxr[:, pos % 4, :], ctxT[:, bass.ds(b * S_PAD, S_PAD)]).then_inc(ctx_in[pos % 4], 16)

            for b in range(4):
                load_ctx(b, b, 0)
            sp.dma_start(cst[:, NFIRST:NCONST], cst_d[:, NFIRST:NCONST]).then_inc(rest_in, 16)
            with sp.Fori(1, NB // 4) as i:
                for u in range(4):
                    load_ctx(4 * i + u, 4 + u, i)
            sp.wait_ge(rest_in, 16)
            rows = sorted_d.rearrange("(j p) r -> p j r", p=128)
            zeros = C("zeros").unsqueeze(1).to_broadcast([128, SLT, D])
            sp.dma_start(rows[:, :, 0:D], zeros).then_inc(pad_out, 16)
            sp.dma_start(rows[:, :, D:2 * D], zeros).then_inc(pad_out, 16)
            sp.dma_start(rows[:, :, 2 * D:ROW], C("pad_tail").rearrange("p (j r) -> p j r", r=2)).then_inc(pad_out, 16)
            sp.dma_start(out_d[TOK:, :].rearrange("(j p) d -> p j d", p=128), zeros).then_inc(pad_out, 16)
            sp.wait_ge(bo_ok, 1)
            sp.wait_ge(qp_ok, 2 * T)
            sp.dma_start(w1all, w1_d).then_inc(w1_in, 16)
            sp.wait_ge(tx_mm, NC)
            sp.wait_ge(r_mm, NC)
            sp.dma_start(w2all, w2_d).then_inc(w2_in, 16)
            sp.wait_ge(sorted_out, 16 * TT)

            def load_tile(j, pos, i):
                if pos >= 4:
                    sp.wait_ge(xt_mm, j - 3)
                    sp.wait_ge(base_ok, j - 3)
                sp.dma_start(sorted_in[:, pos % 4, :], sorted_d[bass.ds(j * 128, 128), :]).then_inc(tile_in[pos % 4], 16)

            per_tile(sp, load_tile)
            for u in range(4):
                sp.wait_ge(stored[u], 16 * ((SLT + 3 - u) // 4))

        @block.tensor
        def _(pe):
            mm, tr = nc.tensor.matmul, nc.tensor.transpose

            def layernorm(s, ready, use):
                for c in range(NC):
                    pe.wait_ge(*ready(c))
                    mm(ln_bank[c][:, :], C("mean"), x[:, cols(c)], start=True, stop=True).then_inc(ln_mean, 1)

                def variance(c):
                    pe.wait_ge(ln_sq, NC * s + c + 1)
                    for k in range(4):
                        last = mm(bank[4 + c % 2][:, k:k + 1], xn[:, cols(4 * c + k, D)], C("mean")[:, 0:1],
                                  start=True, stop=True)
                    last.then_inc(ln_var, 1)

                def spread(c):
                    pe.wait_ge(ln_rstd, NC * s + c + 1)
                    for k in range(4):
                        last = mm(ln_bank[c][:, k * D:(k + 1) * D], rstd[:, 4 * c + k:4 * c + k + 1].to_broadcast([128, D]),
                                  C("ident"), start=True, stop=True)
                    last.then_inc(ln_spread, 1)

                variance(0)
                for c in range(NC):
                    if c + 1 < NC:
                        variance(c + 1)
                    spread(c)
                    if c >= 1:
                        use(c - 1)
                use(NC - 1)

            pe.wait_ge(cst_in, 16)
            def queries(c):
                pe.wait_ge(ln_out, c + 1)
                if c >= 2:
                    pe.wait_ge(q_sb, c - 1)
                mm(bank[c % 2][:, :], C("wq"), xn[:, cols(c)], start=True, stop=True).then_inc(q_mm, 1)

            layernorm(0, lambda c: (x_in[c], 16), lambda c: None)
            for c in range(NC):
                queries(c)

            def K(b, pos, fours):
                pe.wait_ge(ctx_in[pos % 4], 16 * fours)
                if pos >= 1:
                    pe.wait_ge(v_sb, b)
                mm(bank[2][:, 0:S_CTX], C("wk"), ctxr[:, pos % 4, 0:S_CTX], start=True, stop=True).then_inc(k_mm, 1)

            def V(b, pos):
                pe.wait_ge(k_sb, b + 1)
                for c in range(NCH):
                    last = mm(bank[2][0:KCH, c * D:(c + 1) * D], ctxr[:, pos % 4, c * KCH:(c + 1) * KCH], C("wv"),
                              start=True, stop=True)
                last.then_inc(v_mm, 1)

            def scores(b, pos, half):
                if half == 0:
                    pe.wait_ge(k_sb, b + 1)
                    pe.wait_ge(qbd_ok, b + 1)
                if pos >= 1:
                    pe.wait_ge(ex_ok, 2 * b + half - 1)
                for g in (2 * half, 2 * half + 1):
                    r = slice(32 * g, 32 * g + 32)
                    last = mm(bank[4 + g][:, 0:S_CTX], qbd[r, pos % 2, :, :], Ksb[r, pos % 2, :], start=True, stop=True)
                last.then_inc(sc_mm, 1)

            def transposes(b, pos, g):
                pe.wait_ge(pn_ok, 2 * b + g // 2 + 1)
                if pos >= 1 or g >= 2:
                    pe.wait_ge(pt_odd if g % 2 else pt_even, 2 * b + g // 2)
                for c in range(NCH):
                    last = tr(bank[g % 2][0:KCH, c * 128:(c + 1) * 128], P[:, pos % 2, g, c * KCH:(c + 1) * KCH],
                              C("ident"))
                last.then_inc(pt_mm, 1)

            def av(b, pos, g, i):
                if g == 0:
                    pe.wait_ge(v_sb, b + 1)
                    if pos >= 4 and pos % 4 == 0:
                        pe.wait_ge(own_ok, i)
                pe.wait_ge(pt_odd if g % 2 else pt_even, 2 * b + g // 2 + 1)
                for c in range(NCH):
                    last = mm(bank[3][32 * g:32 * g + 32, pos % 4 * 128:pos % 4 * 128 + 128],
                              Vsb[:, pos % 4, c, 32 * g:32 * g + 32], PT[:, g, c, :], start=(c == 0), stop=(c == NCH - 1))
                if g == NG - 1:
                    last.then_inc(av_mm, 1)

            def row(b, pos, i):
                if pos < NB - 1:
                    scores(b + 1, pos + 1, 0)
                if pos >= 1:
                    av(b - 1, pos - 1, 2, i)
                    av(b - 1, pos - 1, 3, i)
                if pos < NB - 2:
                    K(b + 2, pos + 2, i + 1 + (pos % 4 >= 2))
                transposes(b, pos, 0)
                transposes(b, pos, 1)
                if pos < NB - 1:
                    scores(b + 1, pos + 1, 1)
                av(b, pos, 0, i)
                av(b, pos, 1, i)
                if pos < NB - 2:
                    V(b + 2, pos + 2)
                transposes(b, pos, 2)
                transposes(b, pos, 3)

            pe.wait_ge(q_sb, NC)
            pe.wait_ge(pads, 2)
            K(0, 0, 1)
            for half in range(2):
                scores(0, 0, half)
            V(0, 0)
            K(1, 1, 1)
            V(1, 1)
            per_group(pe, row)
            av(NB - 1, NB - 1, 2, 0)
            av(NB - 1, NB - 1, 3, 0)
            pe.wait_ge(rest_in, 16)
            for c in range(NC):
                pe.wait_ge(ot_sb, NB // 4)
                if c >= 2:
                    pe.wait_ge(x1_ok, c - 1)
                mm(bank[c % 2][:, :], C("wo"), qT[:, cols(c)], start=True, stop=True).then_inc(wo_mm, 1)

            def project(c):
                pe.wait_ge(ln_out, NC + c + 1)
                if c >= 2:
                    pe.wait_ge(xp_ok, c - 1)
                mm(bank[c % 2][:, :], C("win"), xn[:, cols(c)], start=True, stop=True).then_inc(in_mm, 1)

            def row_features(u):
                for k in range(4):
                    tok = qT[:, cols(4 * u + k, NB)]
                    for n2 in range(2):
                        last = mm(pair[u % 2][64 * n2:64 * n2 + 64, k // 2, k % 2 * ROWF:(k % 2 + 1) * ROWF], tok,
                                  C(f"wrow{n2}"), start=True, stop=True)
                last.then_inc(row_mm, 1)

            def rows(c):
                pe.wait_ge(xp_ok, c + 1)
                for u in (2 * c, 2 * c + 1):
                    if u >= 2:
                        pe.wait_ge(row_sb, u - 1)
                    row_features(u)

            layernorm(1, lambda c: (x1_ok, c + 1), project)
            for c in range(NC):
                rows(c)

            def retrieve(t, g):
                part = bank[1 + g][:, 0:4 * N_ST]
                pe.wait_ge(p1_ok, 2 * t + g + 1)
                for m in range(0, N_ST, 4):
                    last = mm(part, C("minus"), P1[:, g, :, m:m + 4], start=(m == 0), stop=(m == N_ST - 4))
                    if m == 0:
                        mm(part.rearrange("p (i m) -> p i m", m=4)[:, :, 0], C("ident"),
                           rowf[:, bass.ds(t, 1), 64 + 32 * g:96 + 32 * g].rearrange("p o i -> p (o i)"),
                           start=False, stop=False)
                last.then_inc(pr_mm, 1)

            def readout(t, pos, half):
                if half == 0:
                    pe.wait_ge(qp_ok, 2 * t + 2)
                    if pos >= 1:
                        pe.wait_ge(sq_sb, t)
                for m in range(16 * half, 16 * half + 16, 2):
                    last = mm(bank[3][:, 0:4 * N_ST], C("ident"),
                              QP[:, pos % 2, :, :, m:m + 2].rearrange("p g i j -> p (g i) j"),
                              start=(m == 0), stop=(m == N_ST - 2))
                if half:
                    last.then_inc(sq_mm, 1)

            def step(t, pos):
                for g in range(G2):
                    retrieve(t, g)
                if pos >= 2:
                    for half in range(2):
                        readout(t - 2, pos - 2, half)

            for t in range(4):
                step(t, t)
            with pe.Fori(2, T // 2) as i:
                for u in range(2):
                    step(2 * i + u, 4 + u)
            for t in range(T - 2, T):
                for half in range(2):
                    readout(t, t, half)

            tb = CH // NB

            def sum_halves(c):
                pe.wait_ge(bo_ok, c + 1)
                if c >= 2:
                    pe.wait_ge(bt_sb, c - 1)
                for k in range(tb):
                    last = mm(bank[c % 2][0:G2 * N_ST, k * NB:(k + 1) * NB], KN[:, c * tb + k, :, :], C("sum_halves"),
                              start=True, stop=True)
                last.then_inc(bt_mm, 1)

            def project_out(c):
                pe.wait_ge(bt_sb, c + 1)
                if c >= 2:
                    pe.wait_ge(x2_ok, c - 1)
                mm(bank[4 + c % 2][:, :], cst[0:G2 * N_ST, COL["wout"][0]:COL["wout"][1]], boT[:, c % 2, :],
                   start=True, stop=True).then_inc(y_mm, 1)

            sum_halves(0)
            for c in range(NC):
                if c + 1 < NC:
                    sum_halves(c + 1)
                project_out(c)

            def router(c):
                pe.wait_ge(ln_out, 2 * NC + c + 1)
                for k in range(4 * c, 4 * c + 4):
                    last = mm(bank[0][:, k * E:(k + 1) * E], xn[:, cols(k, D)], C("wr"), start=True, stop=True)
                last.then_inc(r_mm, 1)

            layernorm(2, lambda c: (x2_ok, c + 1), router)
            for c in range(NC):
                if c >= 2:
                    pe.wait_ge(tx_sb, c - 1)
                for k in range(4):
                    last = tr(bank[2 + c % 2][:, k * D:(k + 1) * D], xn[:, cols(4 * c + k, D)], C("ident"))
                last.then_inc(tx_mm, 1)
            pe.wait_ge(best_ok, 1)
            best = eeq[:, :, :].rearrange("p t e -> p (t e)")
            mm(bank[5][:, 0:TT * E], C("before"), best, start=True, stop=True)
            mm(bank[5][:, TT * E:2 * TT * E], C("ones"), best, start=True, stop=True).then_inc(count_mm, 1)
            for c in range(NC):
                if c >= 2:
                    pe.wait_ge(tx_sb, NC + c - 1)
                for k in range(4):
                    last = tr(bank[6 + c % 2][:, k * D:(k + 1) * D], x[:, cols(4 * c + k, D)], C("ident"))
                last.then_inc(tx_mm, 1)
            pe.wait_ge(tx_sb, NC)
            pe.wait_ge(slot_ok, 1)

            def tile_transpose(j, pos, fours):
                pe.wait_ge(tile_in[pos % 4], 16 * fours)
                if pos >= 2:
                    pe.wait_ge(xt_sb, j - 1)
                tr(bank[pos % 2][:, 0:D], sorted_in[:, pos % 4, 0:D], C("ident")).then_inc(xt_mm, 1)

            def hidden(j, pos):
                pe.wait_ge(w_ok, j + 1)
                pe.wait_ge(xt_sb, j + 1)
                for f in range(FC):
                    last = mm(bank[2 + pos % 2][:, f * D:(f + 1) * D], w1s[:, pos % 4, f * D:(f + 1) * D],
                              xTs[:, pos % 2, :], start=True, stop=True)
                last.then_inc(h_mm, 1)

            def result(j, pos):
                pe.wait_ge(h_sb, j + 1)
                if pos >= 2:
                    pe.wait_ge(e_sb, j - 1)
                o = bank[4 + pos % 2][:, 0:D]
                for f in range(FC):
                    last = mm(o, hid[:, pos % 2, f, :], w2s[:, pos % 4, f * D:(f + 1) * D], start=(f == 0),
                              stop=(f == FC - 1))
                last.then_inc(e_mm, 1)

            def tile(j, pos, i):
                if pos < SLT - 1:
                    tile_transpose(j + 1, pos + 1, i + 2 if pos % 4 == 3 else i + 1)
                hidden(j, pos)
                if pos >= 1:
                    result(j - 1, pos - 1)

            tile_transpose(0, 0, 1)
            per_tile(pe, tile)
            result(SLT - 1, SLT - 1)

        @block.scalar
        def _(act):
            af = nc.scalar.activation

            def layernorm(s):
                def square(c):
                    act.wait_ge(ln_cent, NC * s + c + 1)
                    af(xn[:, cols(c)], xc[:, cols(c)], ACT.Square).then_inc(ln_sq, 1)

                square(0)
                for c in range(NC):
                    if c + 1 < NC:
                        square(c + 1)
                    act.wait_ge(ln_var, NC * s + c + 1)
                    af(std[:, 4 * c:4 * c + 4], bank[4 + c % 2][:, 0:4], ACT.Sqrt, bias=C("eps")).then_inc(ln_std, 1)

            act.wait_ge(cst_in, 16)
            layernorm(0)

            def k_out(b, pos):
                act.wait_ge(k_mm, b + 1)
                if pos >= 2:
                    act.wait_ge(sc_mm, 2 * b - 2)
                af(Ksb[:, pos % 2, :], bank[2][:, 0:S_CTX], ACT.Identity, bias=C("bk")).then_inc(k_sb, 1)

            def v_out(b, pos):
                act.wait_ge(v_mm, b + 1)
                nc.scalar.copy(Vsb[:, pos % 4, :, :].rearrange("k c d -> k (c d)"), bank[2][0:KCH, 0:NCH * D]).then_inc(v_sb, 1)

            def exps(b, pos, half):
                act.wait_ge(mx_ok, 2 * b + half + 1)
                if pos >= 2 and half == 0:
                    act.wait_ge(pt_mm, 4 * b - 4)
                for g in (2 * half, 2 * half + 1):
                    last = af(P[:, pos % 2, g, 0:S_CTX], bank[4 + g][:, 0:S_CTX], ACT.Exp,
                              bias=nmx[:, pos % 2, g:g + 1], accum_out=rsum[:, pos % 2, g:g + 1])
                last.then_inc(ex_ok, 1)

            def pt_out(b, g):
                act.wait_ge(pt_mm, 4 * b + g + 1)
                nc.scalar.copy(PT[:, g, :, :].rearrange("k c q -> k (c q)"), bank[1][0:KCH, 0:NCH * 128]).then_inc(pt_odd, 1)

            def row(b, pos, i):
                if pos < NB - 1:
                    exps(b + 1, pos + 1, 0)
                if pos < NB - 2:
                    k_out(b + 2, pos + 2)
                pt_out(b, 1)
                if pos < NB - 1:
                    exps(b + 1, pos + 1, 1)
                if pos < NB - 2:
                    v_out(b + 2, pos + 2)
                pt_out(b, 3)

            act.wait_ge(pads, 2)
            act.wait_ge(q_sb, NC)
            k_out(0, 0)
            v_out(0, 0)
            exps(0, 0, 0)
            k_out(1, 1)
            v_out(1, 1)
            exps(0, 0, 1)
            per_group(act, row)

            layernorm(1)
            for c in range(NC):
                act.wait_ge(in_mm, c + 1)
                af(qT[:, cols(c)], bank[c % 2][:, :], ACT.Silu).then_inc(xp_ok, 1)

            act.wait_ge(prep, NC)
            af(nrm2[:, :], nrm[:, :], ACT.Sqrt).then_inc(prep_sqrt, 1)
            act.wait_ge(prep, NC + 1)
            af(lexp[:, :, :], lsh[:, :, :], ACT.Exp).then_inc(prep_exp, 1)
            act.wait_ge(bias_ok, NC)
            af(BT[:, :, :, :], BT[:, :, :, :], ACT.Sigmoid).then_inc(prep_sig, 1)

            def sq_out(t, pos):
                act.wait_ge(sq_mm, t + 1)
                nc.scalar.copy(SQ2[:, :, bass.ds(t, 1), :].rearrange("p k o x -> p (o x) k"),
                               bank[3][:, 0:4 * N_ST].rearrange("p (x k) -> p x k", k=2)).then_inc(sq_sb, 1)

            def beta_query(t, pos):
                if pos >= 2:
                    act.wait_ge(qp_ok, 2 * t - 2)
                nc.scalar.copy(now[:, pos % 2, 0:2, :], BT[:, bass.ds(t, 1), :, :].rearrange("p o g i -> p (o g) i")).then_inc(step_in, 1)
                nc.scalar.copy(now[:, pos % 2, 2:3, :], rowf[:, bass.ds(t, 1), 192:224]).then_inc(step_in, 1)

            def tanh(t, g):
                act.wait_ge(arg_ok, 2 * t + g + 1)
                ps = pair[g][:, :, :].rearrange("p a f -> p (a f)")
                af(ps, ps, ACT.Tanh).then_inc(tanh_ok, 1)

            def step(t, pos):
                for g in range(G2):
                    act.wait_ge(st_ok, 2 * t + g + 1)
                    af(SP[:, g, :, :], S[:, pos % 2, g, :, :], ACT.Copy,
                       scale=omw[:, bass.ds(t, 1), g])
                tanh(t, 0)
                if pos < T - 1:
                    beta_query(t + 1, pos + 1)
                if pos >= 2:
                    sq_out(t - 2, pos - 2)
                tanh(t, 1)

            act.wait_ge(prep_ok, 1)
            act.wait_ge(prep_sig, 1)
            beta_query(0, 0)
            for t in range(2):
                step(t, t)
            with act.Fori(1, T // 2 - 1) as i:
                for u in range(2):
                    step(2 * i + u, 2 + u)
            for t in range(T - 2, T):
                step(t, t)
            def sigmoid(c):
                act.wait_ge(sq_ok, c + 1)
                r = slice(c * T // NC, (c + 1) * T // NC)
                af(BT[:, r, :, :], SQ[:, r, :, :], ACT.Sigmoid).then_inc(fin_sig, 1)

            def summed_out(c):
                act.wait_ge(bt_mm, c + 1)
                if c >= 2:
                    act.wait_ge(y_mm, c - 1)
                nc.scalar.copy(boT[:, c % 2, :], bank[c % 2][0:G2 * N_ST, :]).then_inc(bt_sb, 1)

            sigmoid(0)
            sq_out(T - 2, T - 2)
            sigmoid(1)
            sigmoid(2)
            sq_out(T - 1, T - 1)
            summed_out(0)
            sigmoid(3)
            for c in range(1, NC):
                summed_out(c)

            layernorm(2)
            act.wait_ge(rt, 2)
            af(eexp[:, :, :], elog[:, :, :], ACT.Exp).then_inc(rt_exp, 1)

            for c in range(NC):
                act.wait_ge(tx_mm, c + 1)
                nc.scalar.copy(tok_row[:, 4 * c:4 * c + 4, 0:D],
                               bank[2 + c % 2][:, :].rearrange("p (k d) -> p k d", k=4)).then_inc(tx_sb, 1)
            for c in range(NC):
                act.wait_ge(tx_mm, NC + c + 1)
                nc.scalar.copy(tok_row[:, 4 * c:4 * c + 4, D:2 * D],
                               bank[6 + c % 2][:, :].rearrange("p (k d) -> p k d", k=4)).then_inc(tx_sb, 1)

            def tile_out(j, pos):
                act.wait_ge(xt_mm, j + 1)
                if pos >= 2:
                    act.wait_ge(h_mm, j - 1)
                nc.scalar.copy(xTs[:, pos % 2, :], bank[pos % 2][:, 0:D]).then_inc(xt_sb, 1)

            def tile(j, pos, i):
                if pos < SLT - 1:
                    tile_out(j + 1, pos + 1)
                act.wait_ge(h_mm, j + 1)
                if pos >= 2:
                    act.wait_ge(e_mm, j - 1)
                for f in range(FC):
                    last = af(hid[:, pos % 2, f, :], bank[2 + pos % 2][:, f * D:(f + 1) * D], ACT.Gelu,
                              bias=b1s[:, pos % 4, f:f + 1])
                last.then_inc(h_sb, 1)

            tile_out(0, 0)
            per_tile(act, tile)

        @block.gpsimd
        def _(pool):
            pool.memset(P[:, :, :, S_CTX:S_PAD], 0.0).then_inc(pads, 1)
            pool.memset(S[:, 0, :, :, :], 0.0).then_inc(pads, 1)
            pool.wait_ge(cst_in, 16)
            pool.wait_ge(q_sb, NC)
            q_tb = qT[:, :].rearrange("p (t b) -> p b t", b=NB)

            def blockdiag(b, pos, i):
                if pos >= 2:
                    pool.wait_ge(sc_mm, 2 * b - 2)
                pool.tensor_tensor(qbd[:, pos % 2, :, :],
                                   q_tb[:, bass.ds(b, 1), :].to_broadcast([D, HG, T]),
                                   C("head_of_row").unsqueeze(2).to_broadcast([D, HG, T]), ALU.mult).then_inc(qbd_ok, 1)

            per_group(pool, blockdiag)
            pool.wait_ge(rest_in, 16)
            for c in range(NC):
                r = slice(c * T // NC, (c + 1) * T // NC)
                sh = [128, T // NC, BLK, BLK]
                kraw = rowf[:, r, 0:64].rearrange("p t (g j) -> p t g j", g=G2)

                def tri(name):
                    return C(name).rearrange("p (n m) -> p n m", m=BLK).unsqueeze(1).to_broadcast(sh)

                pool.wait_ge(row_sb, 2 * c + 2)
                pool.tensor_tensor(KN[:, r, :, :], kraw, kraw, ALU.mult).then_inc(ksq_ok, 1)
                pool.tensor_tensor(BT[:, r, :, :].rearrange("p t g i -> p t (g i)"), rowf[:, r, 128:192],
                                   C("bbeta").unsqueeze(1).to_broadcast([128, T // NC, G2 * N_ST]),
                                   ALU.add).then_inc(bias_ok, 1)
                pool.wait_ge(cmp_ok, 2 * c + 2)
                pool.tensor_tensor(cmpa[:, r, :, :], cmpa[:, r, :, :], tri("low4"), ALU.mult).then_inc(tri_ok, 1)
                pool.tensor_tensor(cmpb[:, r, :, :], cmpb[:, r, :, :], tri("up4"), ALU.mult).then_inc(tri_ok, 1)
                pool.wait_ge(tri_ok, 2 * c + 2)
                pool.tensor_tensor(cmpa[:, r, :, :], cmpa[:, r, :, :], cmpb[:, r, :, :], ALU.add).then_inc(rank_ok, 1)
            pool.wait_ge(prep_ok, 1)

            def beta_state(t, pos):
                pool.wait_ge(step_in, 2 * t + 2)
                for g in range(G2):
                    pool.wait_ge(st_ok, 2 * t + g + 1)
                    if pos >= 1:
                        pool.wait_ge(arg_ok, 2 * t + g - 1)
                    pool.tensor_tensor(A[:, g, :, :], S[:, pos % 2, g, :, :],
                                       now[:, pos % 2, g, :].unsqueeze(2).to_broadcast([128, N_ST, N_ST]),
                                       ALU.mult).then_inc(bs_ok, 1)

            def query_state(t, pos):
                for g in range(G2):
                    pool.wait_ge(st_ok, 2 * t + g + 3)
                    if pos >= 2 and g == 0:
                        pool.wait_ge(sq_mm, t - 1)
                    pool.tensor_tensor(QP[:, pos % 2, g, :, :], S[:, (pos + 1) % 2, g, :, :],
                                       now[:, pos % 2, 2:3, :].to_broadcast([128, N_ST, N_ST]),
                                       ALU.mult).then_inc(qp_ok, 1)

            def step(t, pos):
                if pos < T - 1:
                    beta_state(t + 1, pos + 1)
                query_state(t, pos)

            beta_state(0, 0)
            for t in range(2):
                step(t, t)
            with pool.Fori(1, T // 2 - 1) as i:
                for u in range(2):
                    step(2 * i + u, 2 + u)
            for t in range(T - 2, T):
                step(t, t)

            pool.wait_ge(pad_out, 64)
            pool.wait_ge(tx_sb, 2 * NC)
            pool.wait_ge(row_ok, 2)
            pool.wait_ge(slot_ok, 1)
            for k in range(TT):
                pool.indirect_dma_start(sorted_d, bass.IndirectOffsetOnAxis(slotu[:, k:k + 1], 0),
                                        tok_row[:, k, :], None).then_inc(sorted_out, 16)

            for j in range(SLT):
                pool.wait_ge(e_sb, j + 1)
                pool.indirect_dma_start(out_d, bass.IndirectOffsetOnAxis(dest[:, j:j + 1], 0),
                                        ysb[:, j % 4, :], None).then_inc(stored[j % 4], 16)

        @block.vector
        def _(dve):
            v = nc.vector

            def layernorm(s):
                def centre(c):
                    dve.wait_ge(ln_mean, NC * s + c + 1)
                    v.tensor_tensor(xc[:, cols(c)], x[:, cols(c)], ln_bank[c][:, :], ALU.subtract).then_inc(ln_cent, 1)

                def inverse(c):
                    dve.wait_ge(ln_std, NC * s + c + 1)
                    v.reciprocal(rstd[:, 4 * c:4 * c + 4], std[:, 4 * c:4 * c + 4]).then_inc(ln_rstd, 1)

                def scaled(c):
                    dve.wait_ge(ln_spread, NC * s + c + 1)
                    v.tensor_tensor(xn[:, cols(c)], xc[:, cols(c)], ln_bank[c][:, :], ALU.mult).then_inc(ln_out, 1)

                for c in range(3):
                    centre(c)
                inverse(0)
                centre(3)
                for c in range(1, NC):
                    inverse(c)
                    scaled(c - 1)
                scaled(NC - 1)

            dve.wait_ge(cst_in, 16)
            layernorm(0)
            for c in range(NC):
                dve.wait_ge(q_mm, c + 1)
                v.tensor_scalar(qT[:, cols(c)], bank[c % 2][:, :], C("bq"), DH ** -0.5, ALU.add, ALU.mult).then_inc(q_sb, 1)

            def maxes(b, pos, half):
                dve.wait_ge(sc_mm, 2 * b + half + 1)
                v.tensor_reduce(nmx[:, pos % 2, 2 * half:2 * half + 2], pair[half][:, :, 0:S_CTX], AX.X, ALU.max,
                                negate=True).then_inc(mx_ok, 1)

            def pt_out(b, g):
                dve.wait_ge(pt_mm, 4 * b + g + 1)
                v.tensor_copy(PT[:, g, :, :].rearrange("k c q -> k (c q)"), bank[0][0:KCH, 0:NCH * 128]).then_inc(pt_even, 1)

            def inverse_sums(b, pos, half):
                h = slice(2 * half, 2 * half + 2)
                dve.wait_ge(ex_ok, 2 * b + half + 1)
                v.reciprocal(rinv[:, h], rsum[:, pos % 2, h]).then_inc(rinv_ok, 1)

            def normalise(b, pos, half):
                dve.wait_ge(rinv_ok, 2 * b + half + 1)
                for g in (2 * half, 2 * half + 1):
                    last = v.tensor_scalar(P[:, pos % 2, g, 0:S_CTX], P[:, pos % 2, g, 0:S_CTX], rinv[:, g:g + 1], None,
                                           ALU.mult)
                last.then_inc(pn_ok, 1)

            o_tb = qT[:, :].rearrange("p (t b) -> p b t", b=NB)

            def own_heads(b):
                dve.wait_ge(av_mm, b + 1)
                v.tensor_tensor(avm[:, :].rearrange("p (r h q) -> p r h q", r=4, h=HG),
                                bank[3][:, :].rearrange("p (r h q) -> p r h q", r=4, h=HG),
                                C("head_of_row").unsqueeze(1).unsqueeze(3).to_broadcast([D, 4, HG, T]),
                                ALU.mult).then_inc(own_ok, 1)

            def sum_heads(n):
                dve.wait_ge(own_ok, n)
                v.tensor_reduce(osum[:, :, :], avm[:, :].rearrange("p (r h q) -> p r q h", r=4, h=HG), AX.X,
                                ALU.add).then_inc(osum_ok, 1)

            def heads_out(b, n):
                dve.wait_ge(osum_ok, n)
                v.tensor_scalar(o_tb[:, bass.ds(b - 3, 4), :], osum[:, :, :], C("bv"), None, ALU.add).then_inc(ot_sb, 1)

            def row(b, pos, i):
                if pos < NB - 1:
                    maxes(b + 1, pos + 1, 0)
                four_done = pos % 4 == 0 and pos > 0
                if four_done:
                    own_heads(b - 1)
                pt_out(b, 0)
                if four_done:
                    sum_heads(i)
                if pos < NB - 1:
                    maxes(b + 1, pos + 1, 1)
                    inverse_sums(b + 1, pos + 1, 0)
                if four_done:
                    heads_out(b - 1, i)
                if pos < NB - 1:
                    normalise(b + 1, pos + 1, 0)
                    inverse_sums(b + 1, pos + 1, 1)
                pt_out(b, 2)
                if pos < NB - 1:
                    normalise(b + 1, pos + 1, 1)

            for half in range(2):
                maxes(0, 0, half)
            for half in range(2):
                inverse_sums(0, 0, half)
                normalise(0, 0, half)
            per_group(dve, row)
            dve.wait_ge(rest_in, 16)
            own_heads(NB - 1)
            sum_heads(NB // 4)
            heads_out(NB - 1, NB // 4)
            for c in range(NC):
                dve.wait_ge(wo_mm, c + 1)
                v.scalar_tensor_tensor(x[:, cols(c)], bank[c % 2][:, :], C("bo"), x[:, cols(c)], ALU.add,
                                       ALU.add).then_inc(x1_ok, 1)

            layernorm(1)

            def row_out(u):
                dve.wait_ge(row_mm, u + 1)
                v.tensor_copy(rowf[:, 4 * u:4 * u + 4, :].rearrange("p (a k) f -> p a (k f)", a=2),
                              pair[u % 2][:, :, 0:2 * ROWF]).then_inc(row_sb, 1)

            def squared_norms(c):
                dve.wait_ge(ksq_ok, c + 1)
                n, r = T * G2 // NC, T // NC
                v.tensor_reduce(nrm[:, c * n:(c + 1) * n], KN[:, c * r:(c + 1) * r, :, :].rearrange("p t g j -> p (t g) j"),
                                AX.X, ALU.add).then_inc(prep, 1)

            def compare(c):
                r = slice(c * T // NC, (c + 1) * T // NC)
                sh = [128, T // NC, BLK, BLK]
                logit = rowf[:, r, 224:228]
                higher, before = logit.unsqueeze(2).to_broadcast(sh), logit.unsqueeze(3).to_broadcast(sh)
                dve.wait_ge(row_sb, 2 * c + 2)
                v.tensor_tensor(cmpa[:, r, :, :], higher, before, ALU.is_ge).then_inc(cmp_ok, 1)
                v.tensor_tensor(cmpb[:, r, :, :], higher, before, ALU.is_gt).then_inc(cmp_ok, 1)

            for c in range(NC):
                row_out(2 * c)
                row_out(2 * c + 1)
                compare(c)
                if c >= 1:
                    squared_norms(c - 1)

            chain = [0]

            def made(ins):
                chain[0] += 1
                ins.then_inc(link_ok, 1)
                return chain[0]

            def link(ins):
                dve.wait_ge(link_ok, made(ins))

            logit = rowf[:, :, 224:228]
            dve.wait_ge(row_sb, 2 * NC)
            link(v.tensor_reduce(lmax[:, :], logit, AX.X, ALU.max))
            squared_norms(NC - 1)
            v.tensor_tensor(lsh[:, :, :], logit, lmax[:, :].unsqueeze(2).to_broadcast([128, T, BLK]),
                            ALU.subtract).then_inc(prep, 1)
            dve.wait_ge(rank_ok, NC)
            ranks = made(v.tensor_reduce(rank[:, :, :], cmpa[:, :, :, :], AX.X, ALU.add))
            dve.wait_ge(prep_sqrt, 1)
            norms = made(v.tensor_scalar(nrm3[:, :], nrm2[:, :], 1e-6, None, ALU.add))
            dve.wait_ge(link_ok, ranks)
            v.tensor_scalar(msel[:, :, :], rank[:, :, :], 2.0, None, ALU.is_lt).then_inc(link_ok, 1)
            dve.wait_ge(link_ok, norms)
            v.reciprocal(nrm3[:, :], nrm3[:, :]).then_inc(link_ok, 1)
            chain[0] += 2
            dve.wait_ge(prep_exp, 1)
            link(v.tensor_reduce(lsum[:, :], lexp[:, :, :], AX.X, ALU.add))
            link(v.reciprocal(linv[:, :], lsum[:, :]))
            link(v.tensor_tensor(sm[:, :, :], lexp[:, :, :], linv[:, :].unsqueeze(2).to_broadcast([128, T, BLK]), ALU.mult))
            selected = made(v.tensor_tensor(msel[:, :, :], msel[:, :, :], sm[:, :, :], ALU.mult))
            for n2 in range(2):
                half = slice(64 * n2, 64 * n2 + 64)
                made(v.tensor_copy(smo[half, :, :], sm[half, :, n2::2]))
            dve.wait_ge(link_ok, selected)
            link(v.tensor_reduce(usum[:, :], msel[:, :, :], AX.X, ALU.add))
            link(v.tensor_scalar(usum[:, :], usum[:, :], 1e-8, None, ALU.add))
            link(v.reciprocal(uinv[:, :], usum[:, :]))
            dve.wait_ge(pads, 2)
            for n2 in range(2):
                half = slice(64 * n2, 64 * n2 + 64)
                v.tensor_tensor(wown[half, :, :], msel[half, :, n2::2],
                                uinv[half, :].unsqueeze(2).to_broadcast([64, T, G2]), ALU.mult).then_inc(st_ok, 1)
            dve.wait_ge(st_ok, G2)
            v.tensor_scalar(omw[:, :, :], wown[:, :, :], -1.0, 1.0, ALU.mult, ALU.add).then_inc(prep_ok, 1)

            def flat(ap):
                return ap.rearrange("p i j -> p (i j)")

            def keys(t, pos):
                v.tensor_tensor(bank[0][:, pos % 2 * 64:pos % 2 * 64 + 64].rearrange("p (g j) -> p g j", g=G2),
                                rowf[:, bass.ds(t, 1), 0:64].rearrange("p o (g j) -> p (o g) j", g=G2),
                                nrm3[:, bass.ds(G2 * t, G2)].unsqueeze(2).to_broadcast([128, G2, N_ST]),
                                ALU.mult).then_inc(knp_ok, 1)

            def key_rows(pos, g):
                c = pos % 2 * 64 + g * N_ST
                return bank[0][:, c:c + N_ST].unsqueeze(1).to_broadcast([128, N_ST, N_ST])

            def state_keys(t, pos, g):
                dve.wait_ge(knp_ok, t + 1)
                dve.wait_ge(st_ok, 2 * t + g + 1)
                v.tensor_tensor(P1[:, g, :, :], S[:, pos % 2, g, :, :], key_rows(pos, g), ALU.mult).then_inc(p1_ok, 1)

            def blend(t, pos, g):
                n = 2 * t + g + 1
                dve.wait_ge(tanh_ok, n)
                v.scalar_tensor_tensor(flat(S[:, (pos + 1) % 2, g, :, :]), pair[g][:, :, :].rearrange("p a f -> p (a f)"),
                                       wown[:, bass.ds(t, 1), g], flat(SP[:, g, :, :]), ALU.mult, ALU.add).then_inc(st_ok, 1)

            def delta(t, g):
                dve.wait_ge(pr_mm, 2 * t + g + 1)
                v.tensor_reduce(dlt[:, g, :], bank[1 + g][:, 0:4 * N_ST].rearrange("p (i m) -> p i m", m=4), AX.X,
                                ALU.add).then_inc(dlt_ok, 1)

            def outer(t, pos, g):
                dve.wait_ge(dlt_ok, 2 * t + g + 1)
                v.tensor_tensor(pair[g][:, :, :].rearrange("p a (i j) -> p (a i) j", j=N_ST),
                                dlt[:, g, :].unsqueeze(2).to_broadcast([128, N_ST, N_ST]), key_rows(pos, g),
                                ALU.mult).then_inc(outer_ok, 1)

            def argument(t, g):
                n = 2 * t + g + 1
                dve.wait_ge(outer_ok, n)
                dve.wait_ge(bs_ok, n)
                psg = pair[g][:, :, :].rearrange("p a (i j) -> p (a i) j", j=N_ST)
                v.tensor_tensor(psg, psg, A[:, g, :, :], ALU.add).then_inc(arg_ok, 1)

            def step(t, pos):
                state_keys(t, pos, 0)
                if pos >= 1:
                    blend(t - 1, pos - 1, 1)
                if pos < T - 1:
                    keys(t + 1, pos + 1)
                state_keys(t, pos, 1)
                delta(t, 0)
                outer(t, pos, 0)
                argument(t, 0)
                delta(t, 1)
                outer(t, pos, 1)
                blend(t, pos, 0)
                argument(t, 1)

            keys(0, 0)
            for t in range(4):
                step(t, t)
            with dve.Fori(2, T // 2 - 1) as i:
                for u in range(2):
                    step(2 * i + u, 4 + u)
            for t in range(T - 2, T):
                step(t, t)
            blend(T - 1, T - 1, 1)

            def steps(c):
                return slice(c * T // NC, (c + 1) * T // NC)

            def query_sum(c):
                dve.wait_ge(sq_sb, (c + 1) * T // NC)
                v.tensor_tensor(SQ[:, steps(c), :, :].rearrange("p t g i -> p (t g i)"),
                                SQ2[:, 0, steps(c), :].rearrange("p t x -> p (t x)"),
                                SQ2[:, 1, steps(c), :].rearrange("p t x -> p (t x)"), ALU.add).then_inc(sq_ok, 1)

            def weighted_square(c):
                dve.wait_ge(sq_ok, c + 1)
                v.tensor_tensor(KN[:, steps(c), :, :], SQ[:, steps(c), :, :], SQ[:, steps(c), :, :],
                                ALU.mult).then_inc(sqr_ok, 1)

            def by_router(c):
                dve.wait_ge(sqr_ok, c + 1)
                v.tensor_tensor(KN[:, steps(c), :, :], KN[:, steps(c), :, :],
                                smo[:, steps(c), :].unsqueeze(3).to_broadcast([128, T // NC, G2, N_ST]),
                                ALU.mult).then_inc(wsq_ok, 1)

            def by_sigmoid(c):
                dve.wait_ge(wsq_ok, c + 1)
                dve.wait_ge(fin_sig, c + 1)
                v.tensor_tensor(KN[:, steps(c), :, :], KN[:, steps(c), :, :], BT[:, steps(c), :, :],
                                ALU.mult).then_inc(bo_ok, 1)

            query_sum(0)
            query_sum(1)
            weighted_square(0)
            query_sum(2)
            by_router(0)
            weighted_square(1)
            by_sigmoid(0)
            by_router(1)
            weighted_square(2)
            by_sigmoid(1)
            by_router(2)

            by_sigmoid(2)
            query_sum(3)
            weighted_square(3)
            by_router(3)
            by_sigmoid(3)
            for c in range(NC):
                dve.wait_ge(y_mm, c + 1)
                v.tensor_tensor(x[:, cols(c)], x[:, cols(c)], bank[4 + c % 2][:, :], ALU.add).then_inc(x2_ok, 1)

            layernorm(2)
            dve.wait_ge(r_mm, NC)
            lg = bank[0][:, 0:TT * E].rearrange("p (t e) -> p t e", e=E)
            link(v.tensor_reduce(emax[:, :], lg, AX.X, ALU.max))
            v.tensor_tensor(eeq[:, :, :], lg, emax[:, :].unsqueeze(2).to_broadcast([128, TT, E]), ALU.is_ge).then_inc(rt, 1)
            v.tensor_tensor(elog[:, :, :], lg, emax[:, :].unsqueeze(2).to_broadcast([128, TT, E]), ALU.subtract).then_inc(rt, 1)
            dve.wait_ge(rt, 2)
            link(v.tensor_tensor(eeq[:, :, :], eeq[:, :, :], C("falling").unsqueeze(1).to_broadcast([128, TT, E]), ALU.mult))
            link(v.tensor_reduce(efirst[:, :], eeq[:, :, :], AX.X, ALU.max))
            v.tensor_tensor(eeq[:, :, :], eeq[:, :, :], efirst[:, :].unsqueeze(2).to_broadcast([128, TT, E]),
                            ALU.is_equal).then_inc(best_ok, 1)
            v.tensor_copy(tok_row[:, :, 2 * D:2 * D + 1], C("tok_no").unsqueeze(2)).then_inc(row_ok, 1)
            dve.wait_ge(rt_exp, 1)
            link(v.tensor_reduce(esum[:, :], eexp[:, :, :], AX.X, ALU.add))
            v.reciprocal(tok_row[:, :, 2 * D + 1:ROW], esum[:, :].unsqueeze(2)).then_inc(row_ok, 1)

            dve.wait_ge(count_mm, 1)
            link(v.tensor_copy(tot[:, :, :], bank[5][:, TT * E:2 * TT * E].rearrange("p (t e) -> p t e", e=E)))
            sums, w, at = tot, 1, 0
            while w < TT:
                n = cum[:, at, :, :]
                v.tensor_copy(n[:, 0:w, :], sums[:, 0:w, :]).then_inc(link_ok, 1)
                v.tensor_tensor(n[:, w:TT, :], sums[:, w:TT, :], sums[:, 0:TT - w, :], ALU.add).then_inc(link_ok, 1)
                chain[0] += 2
                dve.wait_ge(link_ok, chain[0])
                sums, w, at = n, 2 * w, 1 - at
            link(v.tensor_tensor(tcmp[:, :, :], sums[:, TT - 1, :].unsqueeze(2).to_broadcast([128, E, TT]),
                                 C("tile_start").unsqueeze(1).to_broadcast([128, E, TT]), ALU.is_gt))
            link(v.tensor_reduce(tiles[:, :], tcmp[:, :, :], AX.X, ALU.add))
            ends, w, at = tiles, 1, 0
            while w < E:
                n = tend[:, at, :]
                v.tensor_copy(n[:, 0:w], ends[:, 0:w]).then_inc(link_ok, 1)
                v.tensor_tensor(n[:, w:E], ends[:, w:E], ends[:, 0:E - w], ALU.add).then_inc(link_ok, 1)
                chain[0] += 2
                dve.wait_ge(link_ok, chain[0])
                ends, w, at = n, 2 * w, 1 - at
            v.tensor_tensor(tbase[:, :], ends[:, :], tiles[:, :], ALU.subtract).then_inc(link_ok, 1)
            v.tensor_tensor(ecmp2[:, :, :], C("tile_no").unsqueeze(2).to_broadcast([128, SLT, E]),
                            ends[:, :].unsqueeze(1).to_broadcast([128, SLT, E]), ALU.is_ge).then_inc(link_ok, 1)
            v.tensor_tensor(epos[:, :, :], sums[:, :, :], tot[:, :, :], ALU.subtract).then_inc(link_ok, 1)
            chain[0] += 3
            dve.wait_ge(link_ok, chain[0])
            v.tensor_reduce(tile_ex[:, :], ecmp2[:, :, :], AX.X, ALU.add).then_inc(link_ok, 1)
            v.tensor_scalar(tbase[:, :], tbase[:, :], float(D), None, ALU.mult).then_inc(link_ok, 1)
            v.tensor_tensor(epos[:, :, :], epos[:, :, :], bank[5][:, 0:TT * E].rearrange("p (t e) -> p t e", e=E),
                            ALU.add).then_inc(link_ok, 1)
            chain[0] += 3
            dve.wait_ge(link_ok, chain[0])
            v.tensor_scalar(tile_ex[:, :], tile_ex[:, :], float(E - 1), None, ALU.min).then_inc(link_ok, 1)
            v.tensor_tensor(epos[:, :, :], epos[:, :, :], tbase[:, :].unsqueeze(1).to_broadcast([128, TT, E]),
                            ALU.add).then_inc(link_ok, 1)
            chain[0] += 2
            dve.wait_ge(link_ok, chain[0])
            v.tensor_copy(tile_exu[:, :], tile_ex[:, :]).then_inc(link_ok, 1)
            v.tensor_tensor(epos[:, :, :], epos[:, :, :], eeq[:, :, :], ALU.mult).then_inc(link_ok, 1)
            chain[0] += 2
            dve.wait_ge(link_ok, chain[0])
            link(v.tensor_reduce(slot[:, :], epos[:, :, :], AX.X, ALU.add))
            v.tensor_copy(slotu[:, :], slot[:, :]).then_inc(slot_ok, 1)

            def prepare(j, pos, fours):
                if pos >= 4:
                    dve.wait_ge(e_sb, j - 3)
                e = dve.value_load(tile_exu[0:1, bass.ds(j, 1)], min_val=0, max_val=E - 1)
                v.tensor_copy(w1s[:, pos % 4, :], w1all[:, bass.ds(e * F, F)])
                v.tensor_copy(b1s[:, pos % 4, :], cst[:, bass.ds(e * FC + COL["b1"][0], FC)])
                v.tensor_copy(w2s[:, pos % 4, :], w2all[:, bass.ds(e * F, F)]).then_inc(w_ok, 1)
                dve.wait_ge(tile_in[pos % 4], 16 * fours)
                r = sorted_in[:, pos % 4, :]
                v.tensor_copy(dest[:, bass.ds(j, 1)], r[:, 2 * D:2 * D + 1])
                v.tensor_copy(prob[:, pos % 4:pos % 4 + 1], r[:, 2 * D + 1:ROW])
                v.scalar_tensor_tensor(base[:, pos % 4, :], cst[:, bass.ds(e * D + COL["b2all"][0], D)],
                                       r[:, 2 * D + 1:ROW], r[:, D:2 * D], ALU.mult, ALU.add).then_inc(base_ok, 1)

            def result_out(j, pos, i):
                if pos >= 4:
                    dve.wait_ge(stored[pos % 4], 16 * i)
                dve.wait_ge(base_ok, j + 1)
                dve.wait_ge(e_mm, j + 1)
                v.scalar_tensor_tensor(ysb[:, pos % 4, :], bank[4 + pos % 2][:, 0:D], prob[:, pos % 4:pos % 4 + 1],
                                       base[:, pos % 4, :], ALU.mult, ALU.add).then_inc(e_sb, 1)

            dve.wait_ge(w1_in, 16)
            dve.wait_ge(w2_in, 16)
            prepare(0, 0, 1)
            prepare(1, 1, 1)

            def tile(j, pos, i):
                if pos < SLT - 2:
                    prepare(j + 2, pos + 2, i + 2 if pos % 4 >= 2 else i + 1)
                result_out(j, pos, i)

            per_tile(dve, tile)


def kernel(x, ctx_1024, L0_xattn_Wq, L0_xattn_bq, L0_xattn_Wk, L0_xattn_bk, L0_xattn_Wv, L0_xattn_bv, L0_xattn_Wo,
           L0_xattn_bo, L0_attn_W_in, L0_attn_W_router, L0_attn_W_kv, L0_attn_W_beta, L0_attn_b_beta, L0_attn_W_q,
           L0_attn_W_out, L0_ffn_Wr, L0_ffn_W1, L0_ffn_b1, L0_ffn_W2, L0_ffn_b2):
    import concourse.bacc as bacc
    from concourse.bass_utils import run_bass_kernel_spmd

    f = np.float32
    n = np.asarray
    xT = n(x).transpose(2, 1, 0).reshape(D, TOK)
    ctxT = np.zeros((D, NB, S_PAD), f)
    ctxT[:, :, :S_CTX] = n(ctx_1024).transpose(2, 0, 1)
    kv = n(L0_attn_W_kv).reshape(BLK, 2, N_ST, D)
    beta = n(L0_attn_W_beta).reshape(BLK, N_ST, D)
    c = np.zeros((128, NCONST), f)

    def put(name, a):
        c[:a.shape[0], COL[name][0]:COL[name][1]] = a

    put("wq", n(L0_xattn_Wq).T)
    put("wk", n(L0_xattn_Wk).T)
    put("wv", n(L0_xattn_Wv).T)
    put("wo", n(L0_xattn_Wo).T)
    put("win", n(L0_attn_W_in).T)
    for h in range(2):
        rows = [kv[h, 0], kv[h + 2, 0], kv[h, 1], kv[h + 2, 1], beta[h], beta[h + 2], n(L0_attn_W_q), n(L0_attn_W_router)]
        put(f"wrow{h}", np.concatenate(rows, 0).T)
    put("wr", n(L0_ffn_Wr))
    p = np.arange(128)
    put("ident", np.eye(128, dtype=f))
    put("minus", -np.eye(128, dtype=f))
    put("mean", np.full((128, 128), 1.0 / D, f))
    put("head_of_row", (p[:, None] // DH % HG == np.arange(HG)).astype(f))
    put("sum_halves", (p[:, None] % NB == np.arange(NB)).astype(f))
    put("bq", n(L0_xattn_bq)[:, None])
    put("bk", n(L0_xattn_bk)[:, None])
    put("bv", n(L0_xattn_bv)[:, None])
    put("bo", n(L0_xattn_bo)[:, None])
    bb = n(L0_attn_b_beta)
    put("bbeta", np.repeat(np.stack([np.concatenate([bb[0], bb[2]]), np.concatenate([bb[1], bb[3]])]), NB, 0))
    put("wout", np.tile(n(L0_attn_W_out).T, (G2, 1)))
    put("low4", np.tile(np.tril(np.ones((4, 4), f), -1).reshape(1, 16), (128, 1)))
    put("up4", np.tile(np.triu(np.ones((4, 4), f), 1).reshape(1, 16), (128, 1)))
    put("falling", np.tile(E - np.arange(E, dtype=f), (128, 1)))
    put("b1", n(L0_ffn_b1).reshape(E * FC, D).T)
    put("b2all", np.tile(n(L0_ffn_b2).reshape(1, E * D), (128, 1)))
    put("before", np.triu(np.ones((128, 128), f), 1))
    put("ones", np.ones((128, 128), f))
    put("tok_no", (p[:, None] + D * np.arange(TT)).astype(f))
    pad = np.zeros((128, SLT, 2), f)
    pad[:, :, 0] = TOK + D * np.arange(SLT) + p[:, None]
    put("pad_tail", pad.reshape(128, SLT * 2))
    put("tile_start", np.tile(D * np.arange(TT, dtype=f), (128, 1)))
    put("tile_no", np.tile(np.arange(SLT, dtype=f), (128, 1)))
    put("eps", np.full((128, 1), 1e-5, f))
    w1 = n(L0_ffn_W1).transpose(1, 0, 2).reshape(D, E * F)
    w2 = n(L0_ffn_W2).reshape(E, FC, D, D).transpose(2, 0, 1, 3).reshape(D, E * FC * D)

    nc = bacc.Bacc("TRN2", target_bir_lowering=False, num_devices=1)
    arrays, args = {}, []
    for name, a in [("xT", xT), ("ctxT", ctxT.reshape(D, NB * S_PAD)), ("cst", c), ("w1", w1), ("w2", w2)]:
        a = np.ascontiguousarray(a)
        arrays[f"in_{name}_dram"] = a
        args.append(nc.dram_tensor(f"in_{name}_dram", a.shape, mybir.dt.from_np(a.dtype), kind="ExternalInput").ap())
    args.append(nc.dram_tensor("out_dram", (TOK + SLT * 128, D), mybir.dt.float32, kind="ExternalOutput").ap())
    args.append(nc.dram_tensor("sorted_dram", (SLT * 128, ROW), mybir.dt.float32, kind="Internal").ap())
    build(nc, *args)
    r = run_bass_kernel_spmd(nc, [arrays], core_ids=[0])
    return np.ascontiguousarray(r.results[0]["out_dram"][:TOK].reshape(T, NB, D).transpose(1, 0, 2))
```
